# Optimizing a Trainium2 kernel written in Bass

```python
import numpy as np
import jax
import jax.numpy as jnp

def _softmax(x, axis=-1):
    return jax.nn.softmax(x, axis=axis)

def _gelu(x):
    return jax.nn.gelu(x, approximate=True)

def _silu(x):
    return jax.nn.silu(x)

def _sigmoid(x):
    return jax.nn.sigmoid(x)

def _layernorm(x, axis=-1, eps=1e-05):
    m = jnp.mean(x, axis=axis, keepdims=True)
    v = jnp.var(x, axis=axis, keepdims=True)
    return (x - m) / jnp.sqrt(v + eps)

def _scatter_add(tgt, idx, src, axis=0):
    return tgt.at[idx].add(src)

def _segment_sum(src, seg, n):
    return jax.ops.segment_sum(src, seg, n)
kernel_name = 'mk_seq_preln_d1_jaxref_r4_77cb8c'

def setup_inputs(seed: int=0):
    np.random.seed(seed)
    _w = jnp.asarray

    def _L0_attn_setup():
        import jax, jax.numpy as jnp
        import numpy as np
        BLOCK = 64
        EPS = 1e-06

        def _silu(x):
            return x * jax.nn.sigmoid(x)
        key = jax.random.key(seed)
        k1, k2, k3, k4 = jax.random.split(key, 4)
        embed_dim, hidden_dim = (512, 512)
        b, n, h = (2, 1024, 16)
        x = jax.random.normal(k1, (b, n, embed_dim), dtype=jnp.float32)
        slope_rate = jax.random.uniform(k2, (h, 1, 1), dtype=jnp.float32, minval=0.01, maxval=1.0)
        W_qkvu = jax.random.normal(k3, (4 * hidden_dim, embed_dim), dtype=jnp.float32) / np.sqrt(embed_dim)
        W_out = jax.random.normal(k4, (embed_dim, hidden_dim), dtype=jnp.float32) / np.sqrt(hidden_dim)
        return {'x': x, 'slope_rate': slope_rate, 'W_qkvu': W_qkvu, 'W_out': W_out}
    _L0_attn_in = _L0_attn_setup()

    def _L0_ffn_setup():
        import jax, jax.numpy as jnp
        import numpy as np
        HIDDEN = 512
        INTER = 1408
        B, S = (2, 512)

        def _ternary(key, shape):
            return jax.random.randint(key, shape, -1, 2).astype(jnp.float32)
        key = jax.random.key(seed)
        ks = jax.random.split(key, 7)
        x = jax.random.normal(ks[0], (B, S, HIDDEN), dtype=jnp.float32)
        gate_w = _ternary(ks[1], (INTER, HIDDEN))
        up_w = _ternary(ks[2], (INTER, HIDDEN))
        down_w = _ternary(ks[3], (HIDDEN, INTER))
        gate_s = jax.random.uniform(ks[4], (INTER,), minval=0.01, maxval=0.1, dtype=jnp.float32)
        up_s = jax.random.uniform(ks[5], (INTER,), minval=0.01, maxval=0.1, dtype=jnp.float32)
        down_s = jax.random.uniform(ks[6], (HIDDEN,), minval=0.01, maxval=0.1, dtype=jnp.float32)
        return {'x': x, 'gate_w': gate_w, 'up_w': up_w, 'down_w': down_w, 'gate_s': gate_s, 'up_s': up_s, 'down_s': down_s}
    _L0_ffn_in = _L0_ffn_setup()
    _d = {'L0_attn_x': _L0_attn_in['x'], 'L0_attn_slope_rate': _L0_attn_in['slope_rate'], 'L0_attn_W_qkvu': _L0_attn_in['W_qkvu'], 'L0_attn_W_out': _L0_attn_in['W_out'], 'L0_ffn_gate_w': _L0_ffn_in['gate_w'], 'L0_ffn_up_w': _L0_ffn_in['up_w'], 'L0_ffn_down_w': _L0_ffn_in['down_w'], 'L0_ffn_gate_s': _L0_ffn_in['gate_s'], 'L0_ffn_up_s': _L0_ffn_in['up_s'], 'L0_ffn_down_s': _L0_ffn_in['down_s']}
    _x0 = _d['L0_attn_x']
    _d['L0_attn_x'] = jax.random.normal(jax.random.fold_in(jax.random.key(seed), 1), (4, 1024, 512), dtype=_x0.dtype)
    del _x0
    return _d

def reference(L0_attn_x, L0_attn_slope_rate, L0_attn_W_qkvu, L0_attn_W_out, L0_ffn_gate_w, L0_ffn_up_w, L0_ffn_down_w, L0_ffn_gate_s, L0_ffn_up_s, L0_ffn_down_s):

    def _L0_attn_ref(x, slope_rate, W_qkvu, W_out):
        import jax, jax.numpy as jnp
        import numpy as np
        BLOCK = 64
        EPS = 1e-06

        def _silu(x):
            return x * jax.nn.sigmoid(x)
        b, n, embed_dim = x.shape
        h = slope_rate.shape[0]
        hidden_dim = W_qkvu.shape[0] // 4
        d = hidden_dim // h
        NB = n // BLOCK
        qkvu = x @ W_qkvu.T
        q, k, v, u = jnp.split(qkvu, 4, axis=-1)

        def to_heads(t):
            return t.reshape(b, n, h, d).transpose(0, 2, 1, 3)
        q = _silu(to_heads(q))
        k = _silu(to_heads(k))
        v = to_heads(v)
        s = slope_rate
        arr = jnp.arange(1, BLOCK + 1, dtype=x.dtype)
        q_decay = jnp.exp(-s * arr[:, None])
        k_decay = jnp.exp(-s * (BLOCK - arr[:, None]))
        idx = arr[:, None] - arr[None, :]
        diag_decay = jnp.exp(jnp.where(idx >= 0, -s * idx, -jnp.inf))
        block_decay = jnp.exp(-s * BLOCK)

        def blk(t):
            return t.reshape(b, h, NB, BLOCK, d).transpose(2, 0, 1, 3, 4)
        qb, kb, vb = (blk(q), blk(k), blk(v))

        def step(kv, inp):
            qi, ki, vi = inp
            qkv_none_diag = jnp.einsum('bhmd,bhde->bhme', qi * q_decay, kv)
            qk = jnp.einsum('bhmd,bhsd->bhms', qi, ki) * diag_decay
            qkv_diag = jnp.einsum('bhms,bhse->bhme', qk, vi)
            kv_new = block_decay * kv + jnp.einsum('bhsd,bhse->bhde', ki * k_decay, vi)
            return (kv_new, qkv_none_diag + qkv_diag)
        kv0 = jnp.zeros((b, h, d, d), dtype=jnp.float32)
        _, outs = jax.lax.scan(step, kv0, (qb, kb, vb))
        o = outs.transpose(1, 2, 0, 3, 4).reshape(b, h, n, d)
        o = o.transpose(0, 2, 1, 3).reshape(b, n, hidden_dim)
        o = o * jax.lax.rsqrt(jnp.mean(o * o, axis=-1, keepdims=True) + EPS)
        o = u * o
        return o @ W_out.T

    def _L0_ffn_ref(x, gate_w, up_w, down_w, gate_s, up_s, down_s):
        import jax, jax.numpy as jnp
        import numpy as np
        HIDDEN = 512
        INTER = 1408
        B, S = (2, 512)

        def _ternary(key, shape):
            return jax.random.randint(key, shape, -1, 2).astype(jnp.float32)
        b, s, h = x.shape
        xf = x.reshape(b * s, h)
        g = jnp.einsum('th,ih->ti', xf, gate_w) * gate_s
        u = jnp.einsum('th,ih->ti', xf, up_w) * up_s
        hdn = jax.nn.silu(g) * u
        out = jnp.einsum('ti,hi->th', hdn, down_w) * down_s
        return out.reshape(b, s, -1)
    x = L0_attn_x
    x = x + _L0_attn_ref(_layernorm(x, axis=-1), L0_attn_slope_rate, L0_attn_W_qkvu, L0_attn_W_out)
    x = x + _L0_ffn_ref(_layernorm(x, axis=-1), L0_ffn_gate_w, L0_ffn_up_w, L0_ffn_down_w, L0_ffn_gate_s, L0_ffn_up_s, L0_ffn_down_s)
    return x

_drawn_inputs = setup_inputs


def setup_inputs(seed=0):
    import zlib

    import numpy as np

    out = dict(_drawn_inputs(seed))
    spreads = {}
    factors = {}
    for name, (base, spread) in spreads.items():
        noise = np.random.default_rng([zlib.crc32(name.encode()), seed]).standard_normal(out[name].shape)
        drawn = base * np.exp(spread * noise) if base else spread * noise
        out[name] = jnp.asarray(drawn.astype(out[name].dtype))
    for name, factor in factors.items():
        out[name] = (out[name] * factor).astype(out[name].dtype)
    return out
```

```python
from contextlib import ExitStack

import concourse.bass as bass
from concourse import mybir

F32 = mybir.dt.float32
F16 = mybir.dt.float16
I32 = mybir.dt.int32
ALU = mybir.AluOpType
ACT = mybir.ActivationFunctionType
AX_X = mybir.AxisListType.X

P = 128
B, T, D = 4, 1024, 512
H, DH = 16, 32
HPG = P // DH
HG = H // HPG
DC = D // P
FF = 1408
FC = FF // P
C = 128
NC = T // C
TB = 2
GT = TB * C
NG = B * T // GT
LN_EPS, RMS_EPS = 1e-5, 1e-6

X_UP = 2.0 ** 10
W_UP = 2.0 ** 14
XW_DOWN = 1.0 / (X_UP * W_UP)
TINY = 2.0 ** -30
EXPONENT = 0x7F800000
MAGNITUDE = 0x7FFFFFFF
RSQRT_SEED = float(0x5F3759DF)

C_IDENT, C_BLOCK, C_REV, C_KEEP = 0, P, 2 * P, 2 * P + 1
N_CONST = C_KEEP + NG
S_REL, S_MASK, S_POS, S_HEAD = (i * P for i in range(4))
N_SETUP = 4 * P

RAW_RING = 8

RING = [("kt", 0, 0), ("down", 0, -1), ("ln1", 0, 1), ("ln1", 1, 1), ("st", 0, 0), ("kt", 1, 0),
        ("q", 0, 1), ("q", 1, 1), ("st", 1, 0), ("down", 1, -1), ("ms", 0, 0), ("k", 0, 1), ("k", 1, 1),
        ("wo", 0, 0), ("wo", 1, 0), ("v", 0, 1), ("v", 1, 1), ("u", 0, 1),
        ("ln2", 0, 0), ("ln2", 1, 0), ("u", 1, 1)] + [("gu", c, 0) for c in range(FC)]
PER = {"kt": 2, "down": 2, "st": 2, "ln1": 2, "ln2": 2, "q": 2, "k": 2, "ms": 1, "v": 2, "wo": 2, "u": 2, "gu": FC}
NBANK = 3


def build_program(nc, x, slope, w_qkvu, w_out, gate_w, up_w, down_w, gate_s, up_s, down_s, consts, setup_consts, out):
    with ExitStack() as ctx:
        def sb(name, shape, dt=F32):
            return ctx.enter_context(nc.sbuf_tensor(name, [P] + shape, dt))

        def sem(name):
            return ctx.enter_context(nc.semaphore(name))

        wq_t = [sb(f"wq_{s}", [DC, 4 * D], F16) for s in ("hi", "lo")]
        wo_t = [sb(f"wo_{s}", [DC, D], F16) for s in ("hi", "lo")]
        wg_t = [sb(f"wg_{s}", [DC, FF], F16) for s in ("hi", "lo")]
        wu_t = [sb(f"wu_{s}", [DC, FF], F16) for s in ("hi", "lo")]
        wd_t = [sb(f"wd_{s}", [FC, D], F16) for s in ("hi", "lo")]
        cst = sb("cst", [N_CONST])
        decay = sb("decay", [HPG, HG, C])
        q_decay = sb("q_decay", [HG, C])
        k_decay = sb("k_decay", [H])
        chunk_decay = sb("chunk_decay", [HG])
        ones = sb("ones", [P])
        v_row = sb("v_row", [D])
        o_row = sb("o_row", [D])
        d_row = sb("d_row", [D])
        nslope = sb("nslope", [H + HG])
        slope_row = sb("slope_row", [H])
        slope_hg = sb("slope_hg", [HG])
        pw_q = sb("pw_q", [16])
        sc_qk = sb("sc_qk", [16])
        pw_g = sb("pw_g", [FC])
        pw_u = sb("pw_u", [FC])
        pw_o = sb("pw_o", [DC])
        pw_d = sb("pw_d", [DC])
        ffn_s = sb("ffn_s", [2, FC])
        down_sc = sb("down_sc", [DC])
        sc_gate = sb("sc_gate", [FC])
        sc_up = sb("sc_up", [FC])
        h_unit = sb("h_unit", [FC])
        small = sb("small", [8, FC])
        x_in = sb("x_in", [TB, D])
        x_res = sb("x_res", [TB, D])
        xn_t = [sb(f"xn_{s}", [DC, GT], F16) for s in ("hi", "lo")]
        g_t = [sb(f"g_{s}", [DC, GT], F16) for s in ("hi", "lo")]
        stats = sb("stats", [2, TB, 6])
        mv = sb("mv", [2, TB, 2])
        ln_y = sb("ln_y", [2, 4, TB])
        wait_slot = sb("wait_slot", [1])
        rms_tok = sb("rms_tok", [5, TB])
        h_row = sb("h_row", [FF])
        arena = sb("arena", [4 * HG * GT + HG * C + D + HPG * HG * C + HG * GT + FC * GT])
        at = [0]

        def carve(shape, dt=F32):
            n = 1
            for s in shape:
                n *= s
            words = n if dt is not F16 else n // 2
            a = arena[:, at[0]:at[0] + words]
            at[0] += words
            if dt is not F32:
                a = a.bitcast(dt)
            if len(shape) == 2:
                a = a.rearrange("p (a b) -> p a b", a=shape[0])
            if len(shape) == 3:
                a = a.rearrange("p (a b c) -> p a b c", a=shape[0], b=shape[1])
            return a

        q_t = carve([HG, GT])
        k_t = carve([HG, GT])
        v = carve([TB, D])
        u_t = carve([HG, GT])
        q_dec = carve([HG, C])
        k_dec = carve([D])
        probs = carve([HPG, HG * C])
        o_t = carve([HG, GT])
        h_t = [carve([FC, GT], F16) for _ in range(2)]
        x2 = sb("x2", [TB, D])
        y_tmp = kv_new = sb("kv_new", [D])
        kv_old = sb("kv_old", [D])
        state = sb("state", [TB, HG, P])
        silu_g = sb("silu_g", [2, GT])
        h32 = sb("h32", [2, GT])
        o_sq = probs[:, 0:2, :].rearrange("p a (h t) -> p (a h) t", h=2)
        rms = probs[:, 2:4, :].rearrange("p a (h t) -> p (a h) t", h=2)
        ring_raw = arena[:, HG * GT * 4:HG * GT * 4 + RAW_RING * D].rearrange("p (n f) -> p n f", n=RAW_RING)
        h_at = HG * GT * 4 + 2 * D + HPG * HG * C + HG * GT
        wo_raw = arena[:, h_at:h_at + DC * D].rearrange("p (n f) -> p n f", n=DC)
        h_raw = arena[:, h_at:h_at + 2 * FF].rearrange("p (n f) -> p n f", n=2)
        probs_raw = arena[:, HG * GT * 4 + 2 * D:HG * GT * 4 + 2 * D + 2 * FF].rearrange("p (n f) -> p n f", n=2)
        u_row = x2[:, 0, :]
        diag = kv_old[:].rearrange("p (n f) -> p n f", n=4)
        scst = arena[:, h_at + DC * D:h_at + DC * D + N_SETUP]

        main = [ctx.enter_context(nc.psum_tensor(f"main{i}", [P, 512], F32)) for i in range(NBANK)]
        sc_ps = [ctx.enter_context(nc.psum_tensor(f"scores{i}", [P, HG * C], F32)) for i in range(HPG)]
        o_ps = ctx.enter_context(nc.psum_tensor("o_ps", [P, HG * C], F32))

        ident = cst[:, C_IDENT:C_IDENT + P]
        rel = scst[:, S_REL:S_REL + P]
        mask = scst[:, S_MASK:S_MASK + P]
        block_mask = cst[:, C_BLOCK:C_BLOCK + P]

        pe = {k: sem(f"pe_{k}") for k in PER}
        pe_scores, pe_o = sem("pe_scores"), sem("pe_o")
        freed = {k: sem(f"{k}_read") for k in PER}
        q_dec_done, probs_done = sem("q_dec_done"), sem("probs_done")
        o_read, o_sq_done, o_sq_sum = sem("o_read"), sem("o_sq_done"), sem("o_sq_sum")
        ln1_hi, ln2_hi, g_hi = sem("ln1_hi"), sem("ln2_hi"), sem("g_hi")
        ln_done = [sem("ln1_done"), sem("ln2_done")]
        ou_done, g_done, g_lo, rms_chain, g_chain = sem("ou_done"), sem("g_done"), sem("g_lo"), sem("rms_chain"), sem("g_chain")
        ln_chain = [sem("ln1_chain"), sem("ln2_chain")]
        st_chain, st_done, y_chain, d_chain = sem("st_chain"), sem("st_done"), sem("y_chain"), sem("d_chain")
        res_added, final = sem("res_added"), sem("final")
        silu_done, h32_done, h_hi, h_lo = sem("silu_done"), sem("h32_done"), sem("h_hi"), sem("h_lo")
        x_loaded, res_loaded, stored = sem("x_loaded"), sem("res_loaded"), sem("stored")
        c_loaded, small_loaded = sem("c_loaded"), sem("small_loaded")
        w_loaded = [sem(f"w_loaded{i}") for i in range(RAW_RING)]
        wo_loaded, wd_loaded = sem("wo_loaded"), [sem(f"wd_loaded{i}") for i in range(DC)]
        setup_done, act_tables, sc_ready = sem("setup_done"), sem("act_tables"), sem("sc_ready")
        s_chain, p_scaled, p_pe, p_hi, p_lo, p_inv = (sem(n) for n in
                                              ("s_chain", "p_scaled", "p_pe", "p_hi", "p_lo", "p_inv"))
        p_mult, rows_ready, tables_done, slopes_ready = (sem(n) for n in ("p_mult", "rows_ready", "tables_done", "slopes_ready"))
        s_pe, s_diag, s_row = sem("s_pe"), sem("s_diag"), sem("s_row")
        free_sem = dict(freed)
        free_sem["gu"] = h32_done

        def present(i, off, kind="body"):
            return not isinstance(i, int) or 0 <= i + off < NG

        def val(kind, i, off, idx):
            return (i + off) * PER[kind] + idx + 1

        def bank_free(eng, k, i):
            j, body = k, i
            for _ in range(2 * len(RING)):
                j -= 1
                if j < 0:
                    j, body = len(RING) - 1, body - 1
                kind, idx, off = RING[j]
                if isinstance(body, int) and body < -1:
                    return
                if j % NBANK == k % NBANK and present(body, off):
                    eng.wait_ge(free_sem[kind], val(kind, body, off, idx))
                    return

        def over(eng, body, last_off=1):
            body(-1)
            body(0)
            with eng.Fori(1, NG - last_off) as i:
                body(i)
            for i in range(NG - last_off, NG + 1):
                body(i)

        GROUPS = []
        for name, w, dst, pw, tiles, most in (("q", w_qkvu, wq_t, pw_q, 16, 4), ("g", gate_w, wg_t, pw_g, FC, 4),
                                              ("u", up_w, wu_t, pw_u, FC, 4), ("o", w_out, wo_t, pw_o, DC, 4),
                                              ("d", down_w, wd_t, pw_d, DC, 1)):
            GROUPS += [(name, w, dst, pw, t0, min(most, tiles - t0)) for t0 in range(0, tiles, most)]
        FIRST = {n: [g[0] for g in GROUPS].index(n) for n in "qguod"}
        TILES_BEFORE = [sum(g[5] for g in GROUPS[:gi]) for gi in range(len(GROUPS) + 1)]
        SETS = [(gi, t, b0, min(4, (FC if g[0] == "d" else DC) - b0)) for gi, g in enumerate(GROUPS)
                for t in range(g[5]) for b0 in range(0, FC if g[0] == "d" else DC, 4)]
        SETS_BEFORE = [sum(1 for s in SETS if s[0] < gi) for gi in range(len(GROUPS) + 1)]

        def sets_of(gi):
            return range(SETS_BEFORE[gi], SETS_BEFORE[gi + 1])

        def raw_tile(gi, t):
            name, t0 = GROUPS[gi][0], GROUPS[gi][4]
            if name == "o":
                return wo_raw[:, t, :]
            if name == "d":
                return (h_raw if t0 < 2 else probs_raw)[:, t0 % 2, :]
            return ring_raw[:, (TILES_BEFORE[gi] + t) % RAW_RING, :]

        def raw_loaded(eng, gi, t):
            name, t0 = GROUPS[gi][0], GROUPS[gi][4]
            n = TILES_BEFORE[gi] + t
            if name == "o":
                eng.wait_ge(wo_loaded, 16)
            elif name == "d":
                eng.wait_ge(wd_loaded[t0], 16)
            else:
                eng.wait_ge(w_loaded[n % RAW_RING], 16 * (n // RAW_RING + 1))

        def is_body(i, n):
            return isinstance(i, int) and i == n

        block = ctx.enter_context(nc.Block())

        x_v = x.rearrange("(b p) (c t) f -> t b (p c) f", b=TB, t=C)
        out_v = out.rearrange("(b p) (c t) f -> t b (p c) f", b=TB, t=C)

        @block.sync
        def _(sp):
            sp.dma_start(x_in[:], x_v[:, :, 0, :]).then_inc(x_loaded, 16)

            def load_tile(n):
                gi = max(g for g in range(len(GROUPS)) if TILES_BEFORE[g] <= n)
                row = (GROUPS[gi][4] + n - TILES_BEFORE[gi]) * P
                sp.dma_start(ring_raw[:, n % RAW_RING, :], GROUPS[gi][1][row:row + P, :]).then_inc(w_loaded[n % RAW_RING], 16)

            for n in range(4):
                load_tile(n)
            sp.dma_start(cst[:], consts).then_inc(c_loaded, 16)
            sp.dma_start(slope_row[0:1, :], slope.rearrange("h a b -> (a b) h")).then_inc(c_loaded, 16)
            sp.dma_start(slope_hg[0:HPG, :], slope.rearrange("(g j) a b -> j (g a b)", j=HPG),
                         allow_slow_non_contiguous=True).then_inc(c_loaded, 16)
            sp.dma_start(scst, setup_consts).then_inc(c_loaded, 16)
            for n in range(4, RAW_RING):
                load_tile(n)
            sp.dma_start(wo_raw, w_out.rearrange("(t p) f -> p t f", p=P)).then_inc(wo_loaded, 16)
            sp.dma_start(ffn_s[:, 0, :], gate_s.rearrange("(c p) -> p c", p=P),
                         allow_slow_non_contiguous=True).then_inc(small_loaded, 16)
            sp.dma_start(ffn_s[:, 1, :], up_s.rearrange("(c p) -> p c", p=P),
                         allow_slow_non_contiguous=True).then_inc(small_loaded, 16)
            sp.dma_start(down_sc[:], down_s.rearrange("(c p) -> p c", p=P),
                         allow_slow_non_contiguous=True).then_inc(small_loaded, 16)
            sp.dma_start(x_res[:], x_v[:, :, 0, :]).then_inc(res_loaded, 16)
            for n in range(RAW_RING, TILES_BEFORE[FIRST["o"]]):
                sp.wait_ge(p_pe, n - RAW_RING + 1)
                load_tile(n)

            def load_down(t):
                sp.dma_start(raw_tile(FIRST["d"] + t, 0), down_w[t * P:(t + 1) * P, :]).then_inc(wd_loaded[t], 16)

            def body(i):
                if is_body(i, 0):
                    sp.wait_ge(p_pe, SETS_BEFORE[FIRST["d"]])
                    sp.wait_ge(tables_done, 1)
                    load_down(0)
                    load_down(1)
                if present(i, 2):
                    sp.wait_ge(pe["ln1"], TB * (i + 1) + TB)
                    sp.dma_start(x_in[:], x_v[:, :, i + 2, :]).then_inc(x_loaded, 16)
                if present(i, -1):
                    sp.wait_ge(final, TB * (i - 1) + TB)
                    sp.dma_start(out_v[:, :, i - 1, :], x2[:]).then_inc(stored, 16)
                if is_body(i, 0):
                    sp.wait_ge(g_lo, 1)
                    load_down(2)
                    load_down(3)
                if present(i, 1) and not is_body(i, -1):
                    sp.wait_ge(pe["ln2"], TB * i + TB)
                    sp.dma_start(x_res[:], x_v[:, :, i + 1, :]).then_inc(res_loaded, 16)

            over(sp, body, 2)
            sp.wait_ge(stored, 16 * NG)

        @block.tensor
        def _(te):
            te.wait_ge(c_loaded, 64)
            te.wait_ge(s_chain, 1)
            nc.tensor.matmul(o_ps[:, 0:H], ones[0:1, :], slope_row[0:1, :], start=True, stop=True)
            nc.tensor.matmul(o_ps[:, H:H + HG], scst[0:HPG, S_HEAD:S_HEAD + P], slope_hg[0:HPG, :],
                             start=True, stop=True, skip_group_check=True).then_inc(s_pe, 1)
            rounds = [0]

            def row_table(cols):
                for c0 in range(0, cols, 4):
                    rounds[0] += 1
                    te.wait_ge(s_diag, rounds[0])
                    for c in range(min(4, cols - c0)):
                        last = nc.tensor.matmul(o_ps[:, c * P:(c + 1) * P], ones[:], diag[:, c, :],
                                                start=True, stop=True, skip_group_check=True)
                    last.then_inc(s_row, 1)

            def transpose_rows(gi):
                for n in sets_of(gi):
                    _, t, b0, nb = SETS[n]
                    te.wait_ge(p_scaled, TILES_BEFORE[gi] + t + 1)
                    if n >= HPG:
                        te.wait_ge(p_lo, n - HPG + 1)
                    if n == SETS_BEFORE[FIRST["d"]]:
                        te.wait_ge(probs_done, TB)
                    for b in range(nb):
                        last = nc.tensor.transpose(sc_ps[n % HPG][:, b * P:(b + 1) * P],
                                                   raw_tile(gi, t)[:, (b0 + b) * P:(b0 + b + 1) * P], ident)
                    last.then_inc(p_pe, 1)

            def setup_before(k, i):
                kind, idx = RING[k][0:2]
                if is_body(i, -1) and idx == 0 and kind in ("q", "k", "v", "u"):
                    g = {"q": 0, "k": 1, "v": 2, "u": 3}[kind]
                    if g == 0:
                        transpose_rows(0)
                    transpose_rows(g + 1)
                    if kind in ("v", "u"):
                        row_table(DC)
                    te.wait_ge(p_lo, SETS_BEFORE[g + 1])
                if is_body(i, 0):
                    if (kind, idx) == ("wo", 0):
                        transpose_rows(FIRST["d"])
                    if (kind, idx) == ("ln2", 0):
                        transpose_rows(FIRST["d"] + 1)
                    if (kind, idx) == ("gu", 4):
                        transpose_rows(FIRST["d"] + 2)
                    if (kind, idx) == ("gu", 8):
                        transpose_rows(FIRST["d"] + 3)

            TERMS = ((0, 0), (0, 1), (1, 0))

            def feature_major(ps, w, a, o0):
                for c in range(DC):
                    for n, (s, m) in enumerate(TERMS):
                        last = nc.tensor.matmul(ps, w[s][:, c, o0:o0 + P], a[m][:, c, :],
                                                start=(c == 0 and n == 0), stop=(c == DC - 1 and n == 2))
                return last

            def token_major(ps, a, b, w, o0, chunks):
                for c in range(chunks):
                    for n, (s, m) in enumerate(TERMS):
                        last = nc.tensor.matmul(ps, a[s][:, c, b * C:(b + 1) * C], w[m][:, c, o0:o0 + D],
                                                start=(c == 0 and n == 0), stop=(c == chunks - 1 and n == 2))
                return last

            def use(k, i):
                kind, idx, off = RING[k]
                if not present(i, off):
                    return
                setup_before(k, i)
                ps = main[k % NBANK]
                bank_free(te, k, i)
                tok = slice(idx * C, (idx + 1) * C)
                if kind == "kt":
                    te.wait_ge(freed["k"], val("k", i, 0, 1))
                    for g in range(HG):
                        last = nc.tensor.transpose(ps[:, g * P:(g + 1) * P], k_t[:, g, tok], ident)
                elif kind in ("ln1", "ln2"):
                    n = 0 if kind == "ln1" else 1
                    te.wait_ge(ln_done[n], TB * (i + off) + idx + 1)
                    for c in range(DC):
                        last = nc.tensor.transpose(ps[:, c * P:(c + 1) * P], (x_in, x_res)[n][:, idx, c * P:(c + 1) * P],
                                                   ident)
                elif kind == "down":
                    te.wait_ge(h_lo, (i - 1) * FC + FC)
                    last = token_major(ps[:], h_t, idx, wd_t, 0, FC)
                elif kind == "st":
                    te.wait_ge(freed["kt"], val("kt", i, 0, idx))
                    for g in range(HG):
                        last = nc.tensor.matmul(ps[:, g * P:(g + 1) * P], k_dec[:, g * P:(g + 1) * P],
                                                v[:, idx, g * P:(g + 1) * P], start=True, stop=True,
                                                skip_group_check=True)
                elif kind in ("q", "k", "u"):
                    te.wait_ge(freed["ln1"], val("ln1", i, 1, 1))
                    base = {"q": 0, "k": D, "u": 3 * D}[kind] + idx * 2 * P
                    for half in range(2):
                        last = feature_major(ps[:, half * GT:(half + 1) * GT], wq_t, xn_t, base + half * P)
                elif kind == "v":
                    te.wait_ge(freed["ln1"], val("ln1", i, 1, 1))
                    last = token_major(ps[:], xn_t, idx, wq_t, 2 * D, DC)
                elif kind == "ms":
                    te.wait_ge(o_sq_sum, i + 1)
                    nc.tensor.matmul(ps[:, 0:GT], ones[:], rms[:, 0, :], start=True, stop=True)
                    for b in range(TB):
                        last = nc.tensor.matmul(ps[:, GT + b:GT + b + 1], rms[:, 0, b * C:(b + 1) * C], ones[:, 0:1],
                                                start=True, stop=True, skip_group_check=True)
                elif kind == "wo":
                    te.wait_ge(g_lo, i + 1)
                    last = token_major(ps[:], g_t, idx, wo_t, 0, DC)
                elif kind == "gu":
                    te.wait_ge(freed["ln2"], val("ln2", i, 0, 1))
                    feature_major(ps[:, 0:GT], wg_t, g_t, idx * P)
                    last = feature_major(ps[:, GT:2 * GT], wu_t, g_t, idx * P)
                last.then_inc(pe[kind], 1)

            def scores(b, i):
                if not present(i, 0):
                    return
                te.wait_ge(freed["q"], val("q", i, 0, 1))
                if b > 0 or not (isinstance(i, int) and i == 0):
                    te.wait_ge(probs_done, TB * i + b)
                tok = slice(b * C, (b + 1) * C)
                for g in range(HG):
                    for j in range(HPG):
                        rows = slice(j * DH, (j + 1) * DH)
                        last = nc.tensor.matmul(sc_ps[j][:, g * C:(g + 1) * C], k_t[rows, g, tok], q_t[rows, g, tok],
                                                start=True, stop=True, skip_group_check=True)
                last.then_inc(pe_scores, 1)

            def outputs(b, i):
                if not present(i, 0):
                    return
                te.wait_ge(q_dec_done, TB * i + b + 1)
                te.wait_ge(probs_done, TB * i + b + 1)
                te.wait_ge(freed["v"], val("v", i, 0, 1))
                if not (isinstance(i, int) and i == 0):
                    te.wait_ge(st_done, TB * (i - 1) + b + 1)
                if b > 0 or not (isinstance(i, int) and i == 0):
                    te.wait_ge(o_read, TB * i + b)
                for g in range(HG):
                    nc.tensor.matmul(o_ps[:, g * C:(g + 1) * C], state[:, b, g, :], q_dec[:, g, :],
                                     start=(g == 0), stop=False, skip_group_check=True)
                for g in range(HG):
                    for j in range(HPG):
                        last = nc.tensor.matmul(o_ps[j * DH:(j + 1) * DH, g * C:(g + 1) * C],
                                                v[:, b, g * P + j * DH:g * P + (j + 1) * DH],
                                                probs[:, j, g * C:(g + 1) * C], start=False, stop=True,
                                                skip_group_check=True)
                last.then_inc(pe_o, 1)

            def body(i):
                for k, (kind, idx, off) in enumerate(RING):
                    if kind == "st":
                        outputs(idx, i)
                    use(k, i)
                    if kind == "kt":
                        scores(idx, i)
                if is_body(i, -1):
                    for g in range(FIRST["g"] + 1, FIRST["d"]):
                        transpose_rows(g)
                    row_table(FC)
                    row_table(DC)
                    te.wait_ge(p_lo, SETS_BEFORE[FIRST["d"]])
                if is_body(i, 0):
                    row_table(DC)
                    te.wait_ge(setup_done, 1)

            over(te, body)

        @block.scalar
        def _(act):
            def decay_tables(part):
                if part == 0:
                    act.wait_ge(slopes_ready, 1)
                for j in ((0, 1), (2, 3), ())[part]:
                    for g in range(HG):
                        h = g * HPG + j
                        nc.scalar.activation(decay[:, j, g, :], rel, ACT.Exp, scale=nslope[:, h:h + 1])
                if part == 2:
                    for g in range(HG):
                        nc.scalar.activation(q_decay[:, g, :], scst[:, S_POS:S_POS + P], ACT.Exp,
                                             scale=nslope[:, H + g:H + g + 1])
                    nc.scalar.activation(chunk_decay[:], nslope[:, H:H + HG], ACT.Exp, scale=float(C))
                    nc.scalar.activation(k_decay[:], nslope[:, 0:H], ACT.Exp,
                                         scale=cst[:, C_REV:C_REV + 1]).then_inc(act_tables, 1)

            def hi_parts(gi):
                _, _, dst, _, t0, _ = GROUPS[gi]
                for n in sets_of(gi):
                    _, t, b0, nb = SETS[n]
                    act.wait_ge(p_pe, n + 1)
                    o0 = (t0 + t) * P
                    nc.scalar.activation(dst[0][:, b0:b0 + nb, o0:o0 + P],
                                         sc_ps[n % HPG][:, 0:nb * P].rearrange("p (b o) -> p b o", b=nb),
                                         ACT.Copy, scale=W_UP).then_inc(p_hi, 1)

            def body(i):
                def product_silus(kind):
                    if not present(i, 1):
                        return
                    dst, base = (q_t, 0) if kind == "q" else (k_t, 4)
                    if is_body(i, -1):
                        if kind == "q":
                            hi_parts(0)
                        hi_parts(1 if kind == "q" else 2)
                        act.wait_ge(sc_ready, 1 if kind == "q" else 2)
                    for idx in range(2):
                        k = RING.index((kind, idx, 1))
                        act.wait_ge(pe[kind], val(kind, i, 1, idx))
                        if idx == 0 and not (isinstance(i, int) and i < 0):
                            act.wait_ge(pe_scores, TB * i + TB)
                            act.wait_ge(q_dec_done, TB * i + TB)
                        for half in range(2):
                            c = 2 * idx + half
                            last = nc.scalar.activation(dst[:, c, :], main[k % NBANK][:, half * GT:(half + 1) * GT],
                                                        ACT.Silu, scale=sc_qk[:, base + c:base + c + 1])
                        last.then_inc(freed[kind], 1)

                def output_out(b):
                    act.wait_ge(pe_o, TB * i + b + 1)
                    ops = o_ps[:].rearrange("p (g t) -> p g t", g=HG)
                    if b == 0 and not (isinstance(i, int) and i == 0):
                        act.wait_ge(g_lo, i)
                    nc.scalar.activation(o_t[:, :, b * C:(b + 1) * C], ops, ACT.Copy).then_inc(o_read, 1)

                if present(i, 1):
                    for t in range(TB):
                        act.wait_ge(pe["ln1"], val("ln1", i, 1, t))
                        if t == 0 and not (isinstance(i, int) and i < 0):
                            act.wait_ge(pe["u"], val("u", i, 0, 1))
                        k = RING.index(("ln1", t, 1))
                        nc.scalar.activation(xn_t[0][:, :, t * C:(t + 1) * C],
                                             main[k % NBANK][:].rearrange("p (c t) -> p c t", c=DC),
                                             ACT.Copy, scale=X_UP).then_inc(ln1_hi, 1)
                if present(i, 0):
                    output_out(0)
                product_silus("q")
                if present(i, 0):
                    output_out(1)
                    act.wait_ge(pe_o, TB * i + TB)
                    act.wait_ge(o_read, TB * i + TB)
                    nc.scalar.activation(o_sq, o_t, ACT.Square).then_inc(o_sq_done, 1)
                if present(i, 0):
                    act.wait_ge(g_done, i + 1)
                    if not (isinstance(i, int) and i == 0):
                        act.wait_ge(pe["gu"], val("gu", i, -1, FC - 1))
                    nc.scalar.activation(g_t[0][:], o_t, ACT.Copy).then_inc(g_hi, 1)
                product_silus("k")
                if is_body(i, 0):
                    hi_parts(FIRST["d"])
                if is_body(i, -1):
                    hi_parts(3)
                    hi_parts(4)
                def u_out(idx):
                    if not present(i, 1):
                        return
                    k = RING.index(("u", idx, 1))
                    act.wait_ge(pe["u"], val("u", i, 1, idx))
                    if idx == 0 and not (isinstance(i, int) and i < 0):
                        act.wait_ge(ou_done, i + 1)
                    nc.scalar.activation(u_t[:, 2 * idx:2 * idx + 2, :],
                                         main[k % NBANK][:].rearrange("p (h t) -> p h t", h=2),
                                         ACT.Copy, scale=XW_DOWN).then_inc(freed["u"], 1)

                u_out(0)
                if is_body(i, -1):
                    u_out(1)
                if is_body(i, -1):
                    for g in range(FIRST["g"] + 1, FIRST["d"]):
                        hi_parts(g)
                        if g <= FIRST["g"] + 3:
                            decay_tables(g - FIRST["g"] - 1)
                if is_body(i, 0):
                    hi_parts(FIRST["d"] + 1)
                if present(i, 0):
                    for t in range(TB):
                        k = RING.index(("ln2", t, 0))
                        act.wait_ge(pe["ln2"], val("ln2", i, 0, t))
                        if t == 0:
                            act.wait_ge(pe["wo"], val("wo", i, 0, 1))
                        nc.scalar.activation(g_t[0][:, :, t * C:(t + 1) * C],
                                             main[k % NBANK][:].rearrange("p (c t) -> p c t", c=DC),
                                             ACT.Copy, scale=X_UP).then_inc(ln2_hi, 1)
                if not is_body(i, -1):
                    u_out(1)
                if present(i, 0):
                    if is_body(i, 0):
                        act.wait_ge(sc_ready, 4)

                    def hidden_hi(c):
                        act.wait_ge(h32_done, i * FC + c + 1)
                        if c == 0 and not (isinstance(i, int) and i == 0):
                            act.wait_ge(pe["down"], val("down", i, -1, 1))
                        nc.scalar.activation(h_t[0][:, c, :], h32[:, c % 2, :], ACT.Copy).then_inc(h_hi, 1)

                    for c in range(FC):
                        k = RING.index(("gu", c, 0))
                        act.wait_ge(pe["gu"], val("gu", i, 0, c))
                        nc.scalar.activation(silu_g[:, c % 2, :], main[k % NBANK][:, 0:GT], ACT.Silu,
                                             scale=sc_gate[:, c:c + 1]).then_inc(silu_done, 1)
                        if c >= 1:
                            hidden_hi(c - 1)
                        if is_body(i, 0) and c in (3, 7):
                            hi_parts(FIRST["d"] + 2 + c // 7)
                    hidden_hi(FC - 1)

            over(act, body)

        @block.vector
        def _(dve):
            ts, tt, stt = nc.vector.tensor_scalar, nc.vector.tensor_tensor, nc.vector.scalar_tensor_tensor
            count = [0]

            def link(ins):
                count[0] += 1
                ins.then_inc(s_chain, 1)
                dve.wait_ge(s_chain, count[0])

            nc.vector.memset(state[:], 0.0)
            link(nc.vector.memset(ones[:], 1.0))

            def row_table(src, cols, dst):
                for c0 in range(0, cols, 4):
                    n = min(4, cols - c0)
                    for c in range(n):
                        last = ts(diag[:, c, :], ident, src[:, c0 + c:c0 + c + 1], None, ALU.mult)
                    last.then_inc(s_diag, 1)
                    rounds[0] += 1
                    dve.wait_ge(s_row, rounds[0])
                    link(nc.vector.tensor_copy(dst[:, c0 * P:(c0 + n) * P], o_ps[:, 0:n * P]))

            rounds = [0]

            def lo_parts(gi):
                _, _, dst, _, t0, _ = GROUPS[gi]
                for n in sets_of(gi):
                    _, t, b0, nb = SETS[n]
                    o0 = (t0 + t) * P
                    dve.wait_ge(p_hi, n + 1)
                    stt(dst[1][:, b0:b0 + nb, o0:o0 + P],
                        sc_ps[n % HPG][:, 0:nb * P].rearrange("p (b o) -> p b o", b=nb), W_UP,
                        dst[0][:, b0:b0 + nb, o0:o0 + P], ALU.mult, ALU.subtract).then_inc(p_lo, 1)

            def power_of_two(dst, src, inv):
                link(ts(dst, src, TINY, None, ALU.max))
                link(ts(dst.bitcast(I32), dst.bitcast(I32), EXPONENT, None, ALU.bitwise_and))
                return nc.vector.reciprocal(inv, dst)

            def row_scales(gi):
                name, _, _, pw, t0, tiles = GROUPS[gi]
                for t in range(tiles):
                    if name in "od":
                        dve.wait_ge(p_mult, t0 + t + 1 + (DC if name == "d" else 0))
                    else:
                        raw_loaded(dve, gi, t)
                    last = nc.vector.tensor_reduce(small[:, 3, t:t + 1], raw_tile(gi, t), axis=AX_X, op=ALU.max,
                                                   apply_absolute_value=True)
                link(last)
                if gi >= 2:
                    dve.wait_ge(p_scaled, TILES_BEFORE[gi - 1])
                power_of_two(pw[:, t0:t0 + tiles], small[:, 3, 0:tiles], small[:, 4 + gi % 2, 0:tiles]).then_inc(p_inv, 1)

            def decay_tables():
                dve.wait_ge(s_pe, 1)
                ts(nslope[:], o_ps[:, 0:H + HG], -1.0, None, ALU.mult).then_inc(slopes_ready, 1)

            def decay_mask():
                dve.wait_ge(act_tables, 1)
                tt(decay[:].rearrange("p j g m -> p (j g) m"), decay[:].rearrange("p j g m -> p (j g) m"),
                   mask.unsqueeze(1).to_broadcast([P, H, C]), ALU.mult).then_inc(tables_done, 1)

            def qkv_scales(g):
                ts(sc_qk[:, 4 * g:4 * g + 4], pw_q[:, 4 * g:4 * g + 4], XW_DOWN, None, ALU.mult).then_inc(sc_ready, 1)

            def ffn_scales():
                dve.wait_ge(small_loaded, 48)
                for s in range(2):
                    link(ts(small[:, s, :].bitcast(I32), ffn_s[:, s, :].bitcast(I32), MAGNITUDE, None, ALU.bitwise_and))
                    link(power_of_two(small[:, s, :], small[:, s, :], small[:, 6 + s, :]))
                link(tt(small[:, 2, :], small[:, 0, :], small[:, 1, :], ALU.mult))
                link(tt(small[:, 2, :], small[:, 2, :], pw_g[:], ALU.mult))
                link(stt(h_unit[:], small[:, 2, :], 2.0 ** 7, pw_u[:], ALU.mult, ALU.mult))
                link(stt(sc_gate[:], pw_g[:], XW_DOWN, ffn_s[:, 0, :], ALU.mult, ALU.mult))
                link(nc.vector.reciprocal(small[:, 2, :], pw_g[:]))
                link(tt(small[:, 2, :], small[:, 2, :], small[:, 6, :], ALU.mult))
                link(tt(small[:, 2, :], small[:, 2, :], small[:, 7, :], ALU.mult))
                stt(sc_up[:], small[:, 2, :], XW_DOWN * 2.0 ** -7, ffn_s[:, 1, :], ALU.mult, ALU.mult).then_inc(sc_ready, 1)

            class Chain:

                def __init__(self, s, n, per):
                    self.s, self.n, self.per, self.k = s, n, per, 0

                def __call__(self, ins):
                    self.k += 1
                    ins.then_inc(self.s, 1)
                    dve.wait_ge(self.s, self.n * self.per + self.k)

                def end(self):
                    assert self.k == self.per

            def rsqrt_guess(link, y, t, vv):
                link(ts(t.bitcast(I32), vv.bitcast(I32), 1, None, ALU.logical_shift_right))
                link(ts(y.bitcast(I32), t.bitcast(I32), -1.0, RSQRT_SEED, ALU.mult, ALU.add))

            def rsqrt_steps(link, y, y0, t, vv):
                for n in range(3):
                    before = y0 if n == 0 else y
                    link(tt(t, before, before, ALU.mult))
                    link(stt(t, t, -0.5, vv, ALU.mult, ALU.mult))
                    link(stt(y, t, 1.5, before, ALU.add, ALU.mult))

            def layer_norm(which, src, dst, n, last):
                link = Chain(ln_chain[which], n, 14)
                st, m = stats[:, which], mv[:, which]
                link(last)
                nc.vector.memset(wait_slot[:], 0.0)
                for b in range(TB):
                    last = nc.vector.bn_aggr(m[:, b, :], st[:, b, :])
                link(last)
                vv, t, y = (ln_y[:, which, r, :] for r in range(3))
                link(ts(vv, m[:, :, 1], LN_EPS, None, ALU.add))
                rsqrt_guess(link, y, t, vv)
                rsqrt_steps(link, y, y, t, vv)
                link.end()
                for b in range(TB):
                    ts(dst[:, b, :], src[:, b, :], m[:, b, 0:1], y[:, b:b + 1],
                       ALU.subtract, ALU.mult).then_inc(ln_done[which], 1)

            def k_decayed(b, i):
                k = RING.index(("kt", b, 0))
                dve.wait_ge(pe["kt"], val("kt", i, 0, b))
                if b > 0 or not (isinstance(i, int) and i == 0):
                    dve.wait_ge(pe["st"], TB * i + b)
                tt(k_dec.rearrange("p (h d) -> p h d", h=H), main[k % NBANK][:].rearrange("p (h d) -> p h d", h=H),
                   k_decay[:].unsqueeze(2).to_broadcast([P, H, DH]), ALU.mult).then_inc(freed["kt"], 1)

            def q_decayed(b, i):
                dve.wait_ge(freed["q"], val("q", i, 0, 1))
                if b > 0 or not (isinstance(i, int) and i == 0):
                    dve.wait_ge(pe_o, TB * i + b)
                tt(q_dec, q_t[:, :, b * C:(b + 1) * C], q_decay[:], ALU.mult).then_inc(q_dec_done, 1)

            def weigh(b, i):
                dve.wait_ge(pe_scores, TB * i + b + 1)
                if not (isinstance(i, int) and i == 0) or b > 0:
                    dve.wait_ge(pe_o, TB * i + b)
                for j in range(HPG):
                    last = tt(probs[:, j, :], sc_ps[j][:], decay[:, j].rearrange("p g m -> p (g m)"), ALU.mult)
                last.then_inc(probs_done, 1)

            def new_state(b, i):
                k = RING.index(("st", b, 0))
                n = TB * i + b
                dve.wait_ge(pe["st"], n + 1)
                if b > 0:
                    dve.wait_ge(st_done, n)
                elif present(i, -1):
                    dve.wait_ge(final, TB * (i - 1) + 1)
                keep = cst[:, bass.ds(C_KEEP + i, 1)]
                stt(kv_new[:].rearrange("p (g e) -> p g e", g=HG), main[k % NBANK][:].rearrange("p (g e) -> p g e", g=HG),
                    keep, block_mask.unsqueeze(1).to_broadcast([P, HG, P]), ALU.mult, ALU.mult).then_inc(freed["st"], 1)
                stt(kv_old[:].rearrange("p (g e) -> p g e", g=HG), state[:, b], keep,
                    chunk_decay[:].unsqueeze(2).to_broadcast([P, HG, P]), ALU.mult, ALU.mult).then_inc(st_chain, 1)
                dve.wait_ge(st_chain, n + 1)
                tt(state[:, b].rearrange("p g e -> p (g e)"), kv_new[:], kv_old[:], ALU.add).then_inc(st_done, 1)

            def down(b, i):
                if not present(i, -1):
                    return
                k = RING.index(("down", b, -1))
                n = TB * (i - 1) + b
                dve.wait_ge(pe["down"], n + 1)
                if b == 0:
                    dve.wait_ge(res_added, TB * i)
                elif present(i, 0):
                    dve.wait_ge(st_done, TB * i + TB)
                else:
                    dve.wait_ge(final, n)
                tt(y_tmp[:], main[k % NBANK][:], d_row[:], ALU.mult).then_inc(freed["down"], 1)
                dve.wait_ge(freed["down"], n + 1)
                tt(x2[:, b, :], x2[:, b, :], y_tmp[:], ALU.add).then_inc(final, 1)

            def token_parts(kind, dst, hi, i, off, t):
                k = RING.index((kind, t, off))
                dve.wait_ge(hi, val(kind, i, off, t))
                stt(dst[1][:, :, t * C:(t + 1) * C], main[k % NBANK][:].rearrange("p (c t) -> p c t", c=DC), X_UP,
                    dst[0][:, :, t * C:(t + 1) * C], ALU.mult, ALU.subtract).then_inc(freed[kind], 1)

            def v_out(idx, i):
                if not present(i, 1):
                    return
                k = RING.index(("v", idx, 1))
                dve.wait_ge(pe["v"], val("v", i, 1, idx))
                if idx == 0 and not (isinstance(i, int) and i < 0):
                    dve.wait_ge(pe["st"], TB * i + TB)
                tt(v[:, idx, :], main[k % NBANK][:], v_row[:], ALU.mult).then_inc(freed["v"], 1)

            def body(i):
                if present(i, 0):
                    k_decayed(0, i)
                    q_decayed(0, i)
                if present(i, 1):
                    dve.wait_ge(x_loaded, 16 * (i + 1) + 16)
                    for b in range(TB):
                        last = nc.vector.bn_stats(stats[:, 0, b, :], x_in[:, b, :])
                    layer_norm(0, x_in, x_in, i + 1, last)
                if present(i, 0):
                    weigh(0, i)
                down(0, i)
                if present(i, 1):
                    if is_body(i, -1):
                        row_scales(0)
                    for t in range(TB):
                        token_parts("ln1", xn_t, ln1_hi, i, 1, t)
                if present(i, 0):
                    new_state(0, i)
                    k_decayed(1, i)
                    q_decayed(1, i)
                    weigh(1, i)
                if is_body(i, -1):
                    decay_tables()
                    row_scales(1)
                    qkv_scales(0)
                    lo_parts(0)
                    row_scales(2)
                    qkv_scales(1)
                    lo_parts(1)
                    row_scales(3)
                    qkv_scales(2)
                    lo_parts(2)
                    dve.wait_ge(sc_ready, 3)
                    row_table(sc_qk[:, 8:12], DC, v_row)
                    row_scales(4)
                    lo_parts(3)
                    row_table(pw_q[:, 12:16], DC, u_row)
                    nc.vector.memset(wait_slot[:], 0.0).then_inc(rows_ready, 1)
                if present(i, 0):
                    new_state(1, i)
                    dve.wait_ge(o_sq_done, i + 1)
                    nc.vector.tensor_reduce(rms[:, 0, :], o_sq.rearrange("p h t -> p t h"), axis=AX_X,
                                            op=ALU.add).then_inc(o_sq_sum, 1)
                    dve.wait_ge(freed["u"], val("u", i, 0, 1))
                    dve.wait_ge(o_read, TB * i + TB)
                    tt(o_t, o_t, u_t, ALU.mult).then_inc(ou_done, 1)
                    if is_body(i, 0):
                        row_scales(FIRST["d"])
                    step = Chain(g_chain, i, 2)
                    dve.wait_ge(pe["ms"], i + 1)
                    k = RING.index(("ms", 0, 0))
                    ts(rms[:, 1, :], main[k % NBANK][:, 0:GT], 1.0 / D, RMS_EPS, ALU.mult, ALU.add)
                    ts(rms_tok[:, 0, :], main[k % NBANK][:, GT:GT + TB], 1.0 / D, RMS_EPS,
                       ALU.mult, ALU.add).then_inc(freed["ms"], 1)
                    dve.wait_ge(freed["ms"], i + 1)
                    rsqrt_guess(step, rms[:, 3, :], rms[:, 2, :], rms[:, 1, :])
                    step.end()
                    dve.wait_ge(ou_done, i + 1)
                    tt(o_t, o_t, rms[:, 3, :].unsqueeze(1).to_broadcast([P, HG, GT]), ALU.mult).then_inc(g_done, 1)
                down(1, i)
                if present(i, 0):
                    dve.wait_ge(g_hi, i + 1)
                    tt(g_t[1][:], o_t, g_t[0][:], ALU.subtract).then_inc(g_lo, 1)
                    step = Chain(rms_chain, i, 13)
                    vv, t, y, y0, f = (rms_tok[:, r, :] for r in range(5))
                    rsqrt_guess(step, y0, t, vv)
                    rsqrt_steps(step, y, y0, t, vv)
                    step(nc.vector.reciprocal(y0, y0))
                    step(tt(f, y, y0, ALU.mult))
                    step.end()
                    if is_body(i, 0):
                        row_scales(FIRST["d"] + 1)
                        lo_parts(FIRST["d"])
                    dve.wait_ge(res_loaded, 16 * i + 16)
                    if not is_body(i, 0):
                        dve.wait_ge(stored, 16 * i)
                    for b in range(TB):
                        k = RING.index(("wo", b, 0))
                        dve.wait_ge(pe["wo"], val("wo", i, 0, b))
                        if b == 0 and present(i, -1):
                            dve.wait_ge(final, TB * (i - 1) + TB)
                        elif b == 0:
                            dve.wait_ge(st_done, TB * i + TB)
                        else:
                            dve.wait_ge(res_added, TB * i + b)
                        tt(y_tmp[:], main[k % NBANK][:], o_row[:], ALU.mult).then_inc(freed["wo"], 1)
                        dve.wait_ge(freed["wo"], val("wo", i, 0, b))
                        stt(x2[:, b, :], y_tmp[:], f[:, b:b + 1], x_res[:, b, :], ALU.mult, ALU.add).then_inc(res_added, 1)
                        dve.wait_ge(res_added, TB * i + b + 1)
                        last = nc.vector.bn_stats(stats[:, 1, b, :], x2[:, b, :])
                    layer_norm(1, x2, x_res, i, last)
                for idx in range(TB):
                    v_out(idx, i)
                if is_body(i, -1):
                    for g in range(FIRST["g"] + 1, FIRST["d"]):
                        row_scales(g)
                        lo_parts(g - 1)
                    lo_parts(FIRST["d"] - 1)
                    decay_mask()
                    ffn_scales()
                    row_table(h_unit[:], FC, h_row)
                    nc.vector.memset(wait_slot[:], 0.0).then_inc(rows_ready, 1)
                    link(ts(pw_o[:], pw_o[:], 1.0 / W_UP, None, ALU.mult))
                    row_table(pw_o[:], DC, o_row)
                if is_body(i, 0):
                    lo_parts(FIRST["d"] + 1)
                if present(i, 0):
                    for t in range(TB):
                        token_parts("ln2", g_t, ln2_hi, i, 0, t)

                    def hidden_lo(c):
                        dve.wait_ge(h_hi, i * FC + c + 1)
                        tt(h_t[1][:, c, :], h32[:, c % 2, :], h_t[0][:, c, :], ALU.subtract).then_inc(h_lo, 1)

                    for c in range(FC):
                        k = RING.index(("gu", c, 0))
                        dve.wait_ge(silu_done, i * FC + c + 1)
                        if c >= 2 or not is_body(i, 0):
                            dve.wait_ge(h_lo, i * FC + max(c - 1, 0))
                        stt(h32[:, c % 2, :], main[k % NBANK][:, GT:2 * GT], sc_up[:, c:c + 1],
                            silu_g[:, c % 2, :], ALU.mult, ALU.mult).then_inc(h32_done, 1)
                        if c >= 1:
                            hidden_lo(c - 1)
                        if is_body(i, 0):
                            if c == 1:
                                row_scales(FIRST["d"] + 2)
                            if c == 4:
                                row_scales(FIRST["d"] + 3)
                                lo_parts(FIRST["d"] + 2)
                            if c == 8:
                                lo_parts(FIRST["d"] + 3)
                    hidden_lo(FC - 1)
                if is_body(i, 0):
                    link(stt(pw_d[:], pw_d[:], 1.0 / W_UP, down_sc[:], ALU.mult, ALU.mult))
                    row_table(pw_d[:], DC, d_row)
                    nc.vector.memset(wait_slot[:], 0.0).then_inc(setup_done, 1)

            over(dve, body)

        @block.gpsimd
        def _(pool):
            mults = [0]
            for gi, (name, _, _, _, t0, tiles) in enumerate(GROUPS):
                if name in "od":
                    pool.wait_ge(rows_ready, 1 if name == "o" else 2)
                    for t in range(tiles):
                        raw_loaded(pool, gi, t)
                        nc.gpsimd.tensor_tensor(raw_tile(gi, t), raw_tile(gi, t), u_row if name == "o" else h_row[:],
                                                ALU.mult).then_inc(p_mult, 1)
                pool.wait_ge(p_inv, gi + 1)
                for t in range(tiles):
                    nc.gpsimd.tensor_scalar(raw_tile(gi, t), raw_tile(gi, t), small[:, 4 + gi % 2, t:t + 1], 1.0,
                                            ALU.mult, ALU.mult).then_inc(p_scaled, 1)


NAMES = {"L0_attn_x": "x", "L0_attn_slope_rate": "slope", "L0_attn_W_qkvu": "w_qkvu", "L0_attn_W_out": "w_out",
         "L0_ffn_gate_w": "gate_w", "L0_ffn_up_w": "up_w", "L0_ffn_down_w": "down_w",
         "L0_ffn_gate_s": "gate_s", "L0_ffn_up_s": "up_s", "L0_ffn_down_s": "down_s"}


def kernel(**inputs):
    import numpy as np
    import concourse.bacc as bacc
    from concourse.bass_utils import run_bass_kernel_spmd

    nc = bacc.Bacc("TRN2", target_bir_lowering=False, num_devices=1)
    arrays = {}
    for name, short in NAMES.items():
        arrays[f"in_{short}"] = np.ascontiguousarray(inputs[name])
    pos = np.arange(P)
    consts = np.zeros((P, N_CONST), np.float32)
    consts[:, C_IDENT:C_IDENT + P] = np.eye(P)
    consts[:, C_BLOCK:C_BLOCK + P] = pos[None, :] // DH == pos[:, None] // DH
    consts[:, C_REV] = C - 1 - pos
    consts[:, C_KEEP:C_KEEP + NG] = np.arange(NG)[None, :] % NC != NC - 1
    setup_consts = np.zeros((P, N_SETUP), np.float32)
    setup_consts[:, S_REL:S_REL + P] = np.maximum(pos[None, :] - pos[:, None], 0)
    setup_consts[:, S_MASK:S_MASK + P] = pos[None, :] >= pos[:, None]
    setup_consts[:, S_POS:S_POS + P] = pos[None, :] + 1
    setup_consts[0:HPG, S_HEAD:S_HEAD + P] = pos[None, :] // DH == np.arange(HPG)[:, None]
    arrays["in_consts"] = consts
    arrays["in_setup_consts"] = setup_consts
    aps = {n: nc.dram_tensor(n, a.shape, mybir.dt.from_np(a.dtype), kind="ExternalInput").ap()
           for n, a in arrays.items()}
    out = nc.dram_tensor("out", (B, T, D), F32, kind="ExternalOutput").ap()
    build_program(nc, *(aps[f"in_{s}"] for s in NAMES.values()), aps["in_consts"],
                  aps["in_setup_consts"], out)
    r = run_bass_kernel_spmd(nc, [arrays], core_ids=[0])
    return r.results[0]["out"]
```

```python
from contextlib import ExitStack

import concourse.bass as bass
from concourse import mybir

F32 = mybir.dt.float32
F16 = mybir.dt.float16
I32 = mybir.dt.int32
ALU = mybir.AluOpType
ACT = mybir.ActivationFunctionType
AX_X = mybir.AxisListType.X

P = 128
B, T, D = 4, 1024, 512
H, DH = 16, 32
HPG = P // DH
HG = H // HPG
DC = D // P
FF = 1408
FC = FF // P
C = 128
NC = T // C
TB = 2
GT = TB * C
NG = B * T // GT
LN_EPS, RMS_EPS = 1e-5, 1e-6

X_UP = 2.0 ** 10
W_UP = 2.0 ** 14
XW_DOWN = 1.0 / (X_UP * W_UP)
TINY = 2.0 ** -30
EXPONENT = 0x7F800000
MAGNITUDE = 0x7FFFFFFF
RSQRT_SEED = float(0x5F3759DF)

C_IDENT, C_BLOCK, C_REV, C_KEEP = 0, P, 2 * P, 2 * P + 1
N_CONST = C_KEEP + NG
S_REL, S_MASK, S_POS, S_HEAD = (i * P for i in range(4))
N_SETUP = 4 * P

RAW_RING = 8

RING = [("kt", 0, 0), ("down", 0, -1), ("ln1", 0, 1), ("ln1", 1, 1), ("st", 0, 0), ("kt", 1, 0),
        ("q", 0, 1), ("q", 1, 1), ("st", 1, 0), ("down", 1, -1), ("ms", 0, 0), ("k", 0, 1), ("k", 1, 1),
        ("wo", 0, 0), ("wo", 1, 0), ("v", 0, 1), ("v", 1, 1), ("u", 0, 1),
        ("ln2", 0, 0), ("ln2", 1, 0), ("u", 1, 1)] + [("gu", c, 0) for c in range(FC)]
PER = {"kt": 2, "down": 2, "st": 2, "ln1": 2, "ln2": 2, "q": 2, "k": 2, "ms": 1, "v": 2, "wo": 2, "u": 2, "gu": FC}
NBANK = 3
SCORES_AT, MS_AT = 2, 7
assert RING[RING.index(("down", 1, -1)) + 1][0] == "ms"


def build_program(nc, x, slope, w_qkvu, w_out, gate_w, up_w, down_w, gate_s, up_s, down_s, consts, setup_consts, out):
    with ExitStack() as ctx:
        def sb(name, shape, dt=F32):
            return ctx.enter_context(nc.sbuf_tensor(name, [P] + shape, dt))

        def sem(name):
            return ctx.enter_context(nc.semaphore(name))

        wq_t = [sb(f"wq_{s}", [DC, 4 * D], F16) for s in ("hi", "lo")]
        wo_t = [sb(f"wo_{s}", [DC, D], F16) for s in ("hi", "lo")]
        wg_t = [sb(f"wg_{s}", [DC, FF], F16) for s in ("hi", "lo")]
        wu_t = [sb(f"wu_{s}", [DC, FF], F16) for s in ("hi", "lo")]
        wd_t = [sb(f"wd_{s}", [FC, D], F16) for s in ("hi", "lo")]
        cst = sb("cst", [N_CONST])
        decay = sb("decay", [HPG, HG, C])
        q_decay = sb("q_decay", [HG, C])
        k_decay = sb("k_decay", [H])
        chunk_decay = sb("chunk_decay", [HG])
        ones = sb("ones", [P])
        v_row = sb("v_row", [D])
        o_row = sb("o_row", [D])
        d_row = sb("d_row", [D])
        nslope = sb("nslope", [H + HG])
        slope_row = sb("slope_row", [H])
        slope_hg = sb("slope_hg", [HG])
        pw_q = sb("pw_q", [16])
        sc_qk = sb("sc_qk", [16])
        pw_g = sb("pw_g", [FC])
        pw_u = sb("pw_u", [FC])
        pw_o = sb("pw_o", [DC])
        pw_d = sb("pw_d", [DC])
        ffn_s = sb("ffn_s", [2, FC])
        down_sc = sb("down_sc", [DC])
        sc_gate = sb("sc_gate", [FC])
        sc_up = sb("sc_up", [FC])
        h_unit = sb("h_unit", [FC])
        small = sb("small", [8, FC])
        x_in = sb("x_in", [TB, D])
        x_res = sb("x_res", [TB, D])
        xn_t = [sb(f"xn_{s}", [DC, GT], F16) for s in ("hi", "lo")]
        g_t = [sb(f"g_{s}", [DC, GT], F16) for s in ("hi", "lo")]
        stats = sb("stats", [2, TB, 6])
        mv = sb("mv", [2, TB, 2])
        ln_y = sb("ln_y", [2, 4, TB])
        wait_slot = sb("wait_slot", [1])
        rms_tok = sb("rms_tok", [5, TB])
        h_row = sb("h_row", [FF])
        arena = sb("arena", [4 * HG * GT + HG * C + D + HPG * HG * C + HG * GT + FC * GT])
        at = [0]

        def carve(shape, dt=F32):
            n = 1
            for s in shape:
                n *= s
            words = n if dt is not F16 else n // 2
            a = arena[:, at[0]:at[0] + words]
            at[0] += words
            if dt is not F32:
                a = a.bitcast(dt)
            if len(shape) == 2:
                a = a.rearrange("p (a b) -> p a b", a=shape[0])
            if len(shape) == 3:
                a = a.rearrange("p (a b c) -> p a b c", a=shape[0], b=shape[1])
            return a

        q_t = carve([HG, GT])
        k_t = carve([HG, GT])
        v = carve([TB, D])
        u_t = carve([HG, GT])
        q_dec = carve([HG, C])
        k_dec = carve([D])
        probs = carve([HPG, HG * C])
        o_t = carve([HG, GT])
        h_t = [carve([FC, GT], F16) for _ in range(2)]
        x2 = sb("x2", [TB, D])
        y_tmp = kv_new = sb("kv_new", [D])
        kv_old = sb("kv_old", [D])
        state = sb("state", [TB, HG, P])
        silu_g = sb("silu_g", [2, GT])
        h32 = sb("h32", [2, GT])
        o_sq = probs[:, 0:2, :].rearrange("p a (h t) -> p (a h) t", h=2)
        rms = probs[:, 2:4, :].rearrange("p a (h t) -> p (a h) t", h=2)
        ring_raw = arena[:, HG * GT * 4:HG * GT * 4 + RAW_RING * D].rearrange("p (n f) -> p n f", n=RAW_RING)
        h_at = HG * GT * 4 + 2 * D + HPG * HG * C + HG * GT
        h_raw = arena[:, h_at:h_at + 2 * FF].rearrange("p (n f) -> p n f", n=2)
        probs_raw = arena[:, HG * GT * 4 + 2 * D:HG * GT * 4 + 2 * D + 2 * FF].rearrange("p (n f) -> p n f", n=2)
        u_row = x2[:, 0, :]
        scst = arena[:, h_at:h_at + N_SETUP]

        main = [ctx.enter_context(nc.psum_tensor(f"main{i}", [P, 512], F32)) for i in range(NBANK)]
        sc_ps = [ctx.enter_context(nc.psum_tensor(f"scores{i}", [P, HG * C], F32)) for i in range(HPG)]
        o_ps = ctx.enter_context(nc.psum_tensor("o_ps", [P, HG * C], F32))

        ident = cst[:, C_IDENT:C_IDENT + P]
        rel = scst[:, S_REL:S_REL + P]
        mask = scst[:, S_MASK:S_MASK + P]
        block_mask = cst[:, C_BLOCK:C_BLOCK + P]

        pe = {k: sem(f"pe_{k}") for k in PER}
        pe_scores, pe_o = sem("pe_scores"), sem("pe_o")
        freed = {k: sem(f"{k}_read") for k in PER}
        q_dec_done, probs_done = sem("q_dec_done"), sem("probs_done")
        o_read, o_sq_done, o_sq_sum = sem("o_read"), sem("o_sq_done"), sem("o_sq_sum")
        ln1_hi, ln2_hi, g_hi = sem("ln1_hi"), sem("ln2_hi"), sem("g_hi")
        ln_done = [sem("ln1_done"), sem("ln2_done")]
        ou_done, g_done, g_lo = sem("ou_done"), sem("g_done"), sem("g_lo")
        rms_chain, g_chain = sem("rms_chain"), sem("g_chain")
        ln_chain = [sem("ln1_chain"), sem("ln2_chain")]
        st_chain, st_done, y_chain, d_chain = sem("st_chain"), sem("st_done"), sem("y_chain"), sem("d_chain")
        res_added, final = sem("res_added"), sem("final")
        silu_done, h32_done, h_hi, h_lo = sem("silu_done"), sem("h32_done"), sem("h_hi"), sem("h_lo")
        x_loaded, res_loaded, stored = sem("x_loaded"), sem("res_loaded"), sem("stored")
        c_loaded, small_loaded = sem("c_loaded"), sem("small_loaded")
        w_loaded = [sem(f"w_loaded{i}") for i in range(RAW_RING)]
        wd_loaded = [sem(f"wd_loaded{i}") for i in range(DC)]
        act_tables, sc_ready = sem("act_tables"), sem("sc_ready")
        setup_chain, scales_ready, rows_scaled = sem("setup_chain"), sem("scales_ready"), sem("rows_scaled")
        rows_transposed, weights_hi, weights_lo = sem("rows_transposed"), sem("weights_hi"), sem("weights_lo")
        columns_scaled, tables_done, slopes_ready = sem("columns_scaled"), sem("tables_done"), sem("slopes_ready")
        slopes_spread, row_made, row_copied = sem("slopes_spread"), sem("row_made"), sem("row_copied")
        free_sem = dict(freed)
        free_sem["gu"] = h32_done

        def present(i, off):
            return not isinstance(i, int) or 0 <= i + off < NG

        def val(kind, i, off, idx):
            return (i + off) * PER[kind] + idx + 1

        def bank_free(eng, k, i):
            j, body = k, i
            for _ in range(2 * len(RING)):
                j -= 1
                if j < 0:
                    j, body = len(RING) - 1, body - 1
                kind, idx, off = RING[j]
                if isinstance(body, int) and body < -1:
                    return
                if j % NBANK == k % NBANK and present(body, off):
                    eng.wait_ge(free_sem[kind], val(kind, body, off, idx))
                    return

        def over(eng, body, last_off=1):
            body(-1)
            body(0)
            with eng.Fori(1, NG - last_off) as i:
                body(i)
            for i in range(NG - last_off, NG + 1):
                body(i)

        SOURCES = {"q": (w_qkvu, wq_t, pw_q, 16, 4), "g": (gate_w, wg_t, pw_g, FC, 4), "u": (up_w, wu_t, pw_u, FC, 4),
                   "o": (w_out, wo_t, pw_o, DC, 4), "d": (down_w, wd_t, pw_d, DC, 1)}
        ORDER = (("q", 0), ("q", 4), ("q", 8), ("q", 12), ("g", 0), ("g", 4), ("o", 0), ("g", 8),
                 ("u", 0), ("u", 4), ("u", 8)) + tuple(("d", t) for t in range(DC))
        GROUPS = [(n,) + SOURCES[n][0:3] + (t0, min(SOURCES[n][4], SOURCES[n][3] - t0)) for n, t0 in ORDER]
        FIRST = {n: [g[0] for g in GROUPS].index(n) for n in "qguod"}
        TILES_BEFORE = [sum(g[5] for g in GROUPS[:gi]) for gi in range(len(GROUPS) + 1)]
        SETS = [(gi, t, b0, min(4, (FC if g[0] == "d" else DC) - b0)) for gi, g in enumerate(GROUPS)
                for t in range(g[5]) for b0 in range(0, FC if g[0] == "d" else DC, 4)]
        SETS_BEFORE = [sum(1 for s in SETS if s[0] < gi) for gi in range(len(GROUPS) + 1)]

        TABLES = (("v", DC), ("u", DC), ("o", DC), ("h", FC), ("d", DC))
        ROUNDS = {n: sum(-(-m // 4) for _, m in TABLES[:t + 1]) for t, (n, _) in enumerate(TABLES)}

        def sets_of(gi):
            return range(SETS_BEFORE[gi], SETS_BEFORE[gi + 1])

        def raw_tile(gi, t):
            name, t0 = GROUPS[gi][0], GROUPS[gi][4]
            if name == "d":
                return (h_raw if t0 < 2 else probs_raw)[:, t0 % 2, :]
            return ring_raw[:, (TILES_BEFORE[gi] + t) % RAW_RING, :]

        def raw_loaded(eng, gi, t):
            name, t0 = GROUPS[gi][0], GROUPS[gi][4]
            n = TILES_BEFORE[gi] + t
            if name == "d":
                eng.wait_ge(wd_loaded[t0], 16)
            else:
                eng.wait_ge(w_loaded[n % RAW_RING], 16 * (n // RAW_RING + 1))

        def is_body(i, n):
            return isinstance(i, int) and i == n

        block = ctx.enter_context(nc.Block())

        x_v = x.rearrange("(b p) (c t) f -> t b (p c) f", b=TB, t=C)
        out_v = out.rearrange("(b p) (c t) f -> t b (p c) f", b=TB, t=C)

        @block.sync
        def _(sp):
            sp.dma_start(x_in[:], x_v[:, :, 0, :]).then_inc(x_loaded, 16)

            def load_tile(n):
                gi = max(g for g in range(len(GROUPS)) if TILES_BEFORE[g] <= n)
                row = (GROUPS[gi][4] + n - TILES_BEFORE[gi]) * P
                sp.dma_start(ring_raw[:, n % RAW_RING, :], GROUPS[gi][1][row:row + P, :]).then_inc(w_loaded[n % RAW_RING], 16)

            for n in range(4):
                load_tile(n)
            sp.dma_start(cst[:], consts).then_inc(c_loaded, 16)
            sp.dma_start(slope_row[0:1, :], slope.rearrange("h a b -> (a b) h")).then_inc(c_loaded, 16)
            sp.dma_start(slope_hg[0:HPG, :], slope.rearrange("(g j) a b -> j (g a b)", j=HPG),
                         allow_slow_non_contiguous=True).then_inc(c_loaded, 16)
            sp.dma_start(scst, setup_consts).then_inc(c_loaded, 16)
            for n in range(4, RAW_RING):
                load_tile(n)
            sp.dma_start(ffn_s[:, 0, :], gate_s.rearrange("(c p) -> p c", p=P),
                         allow_slow_non_contiguous=True).then_inc(small_loaded, 16)
            sp.dma_start(ffn_s[:, 1, :], up_s.rearrange("(c p) -> p c", p=P),
                         allow_slow_non_contiguous=True).then_inc(small_loaded, 16)
            sp.dma_start(down_sc[:], down_s.rearrange("(c p) -> p c", p=P),
                         allow_slow_non_contiguous=True).then_inc(small_loaded, 16)
            sp.dma_start(x_res[:], x_v[:, :, 0, :]).then_inc(res_loaded, 16)
            for n in range(RAW_RING, TILES_BEFORE[FIRST["d"]]):
                if n == 2 * RAW_RING:
                    sp.wait_ge(pe["ln1"], TB)
                    sp.dma_start(x_in[:], x_v[:, :, 1, :]).then_inc(x_loaded, 16)
                sp.wait_ge(rows_transposed, n - RAW_RING + 1)
                load_tile(n)

            def load_down(t):
                sp.dma_start(raw_tile(FIRST["d"] + t, 0), down_w[t * P:(t + 1) * P, :]).then_inc(wd_loaded[t], 16)

            def body(i):
                if is_body(i, 0):
                    sp.wait_ge(rows_transposed, SETS_BEFORE[FIRST["d"]])
                    sp.wait_ge(tables_done, 1)
                    load_down(0)
                    load_down(1)
                if present(i, 2) and not is_body(i, -1):
                    sp.wait_ge(pe["ln1"], TB * (i + 1) + TB)
                    sp.dma_start(x_in[:], x_v[:, :, i + 2, :]).then_inc(x_loaded, 16)
                if present(i, -1):
                    sp.wait_ge(final, TB * (i - 1) + TB)
                    sp.dma_start(out_v[:, :, i - 1, :], x2[:]).then_inc(stored, 16)
                if is_body(i, 0):
                    sp.wait_ge(g_lo, TB)
                    load_down(2)
                    load_down(3)
                if present(i, 1) and not is_body(i, -1):
                    sp.wait_ge(pe["ln2"], TB * i + TB)
                    sp.dma_start(x_res[:], x_v[:, :, i + 1, :]).then_inc(res_loaded, 16)

            over(sp, body, 2)
            sp.wait_ge(stored, 16 * NG)

        @block.tensor
        def _(te):
            te.wait_ge(c_loaded, 64)
            te.wait_ge(setup_chain, 1)
            nc.tensor.matmul(o_ps[:, 0:H], ones[0:1, :], slope_row[0:1, :], start=True, stop=True)
            nc.tensor.matmul(o_ps[:, H:H + HG], scst[0:HPG, S_HEAD:S_HEAD + P], slope_hg[0:HPG, :],
                             start=True, stop=True, skip_group_check=True).then_inc(slopes_spread, 1)
            rounds = [0]

            def row_table(src, cols, banks=(o_ps,)):
                for n, c0 in enumerate(range(0, cols, 4)):
                    if len(banks) == 1 and rounds[0]:
                        te.wait_ge(row_copied, rounds[0])
                    for c in range(min(4, cols - c0)):
                        last = nc.tensor.matmul(banks[n][:, c * P:(c + 1) * P],
                                                src[:, c0 + c:c0 + c + 1].to_broadcast([P, P]), ident,
                                                start=True, stop=True, skip_group_check=True)
                    last.then_inc(row_made, 1)
                    rounds[0] += 1

            def transpose_rows(gi):
                for n in sets_of(gi):
                    _, t, b0, nb = SETS[n]
                    te.wait_ge(rows_scaled, TILES_BEFORE[gi] + t + 1)
                    if n >= HPG:
                        te.wait_ge(weights_lo, n - HPG + 1)
                    if n == SETS_BEFORE[FIRST["d"]]:
                        te.wait_ge(probs_done, TB)
                    for b in range(nb):
                        last = nc.tensor.transpose(sc_ps[n % HPG][:, b * P:(b + 1) * P],
                                                   raw_tile(gi, t)[:, (b0 + b) * P:(b0 + b + 1) * P], ident)
                    last.then_inc(rows_transposed, 1)

            def setup_before(k, i):
                kind, idx = RING[k][0:2]
                if is_body(i, -1) and idx == 0 and kind in ("q", "k", "v", "u"):
                    g = {"q": 0, "k": 1, "v": 2, "u": 3}[kind]
                    if g == 0:
                        transpose_rows(0)
                    if kind == "v":
                        te.wait_ge(sc_ready, 3)
                        te.wait_ge(slopes_ready, 1)
                        row_table(sc_qk[:, 8:12], DC)
                    transpose_rows(g + 1)
                    if kind == "v":
                        te.wait_ge(scales_ready, 4)
                        row_table(pw_q[:, 12:16], DC)
                    te.wait_ge(weights_lo, SETS_BEFORE[g + 1])
                if is_body(i, 0):
                    if (kind, idx) == ("ms", 0):
                        transpose_rows(FIRST["d"])
                    if (kind, idx) == ("ln2", 0):
                        transpose_rows(FIRST["d"] + 1)
                    if (kind, idx) == ("gu", 4):
                        transpose_rows(FIRST["d"] + 2)
                    if (kind, idx) == ("gu", 8):
                        transpose_rows(FIRST["d"] + 3)

            TERMS = ((0, 0), (0, 1), (1, 0))

            def feature_major(ps, w, a, o0):
                for c in range(DC):
                    for n, (s, m) in enumerate(TERMS):
                        last = nc.tensor.matmul(ps, w[s][:, c, o0:o0 + P], a[m][:, c, :],
                                                start=(c == 0 and n == 0), stop=(c == DC - 1 and n == 2))
                return last

            def token_major(ps, a, b, w, o0, chunks, part=None):
                for c in part or range(chunks):
                    for n, (s, m) in enumerate(TERMS):
                        last = nc.tensor.matmul(ps, a[s][:, c, b * C:(b + 1) * C], w[m][:, c, o0:o0 + D],
                                                start=(c == 0 and n == 0), stop=(c == chunks - 1 and n == 2))
                return last

            def use(k, i):
                kind, idx, off = RING[k]
                if not present(i, off):
                    return
                setup_before(k, i)
                ps = main[k % NBANK]
                bank_free(te, k, i)
                tok = slice(idx * C, (idx + 1) * C)
                if kind == "kt":
                    te.wait_ge(freed["k"], val("k", i, 0, 1))
                    for g in range(HG):
                        last = nc.tensor.transpose(ps[:, g * P:(g + 1) * P], k_t[:, g, tok], ident)
                elif kind in ("ln1", "ln2"):
                    n = 0 if kind == "ln1" else 1
                    te.wait_ge(ln_done[n], TB * (i + off) + idx + 1)
                    for c in range(DC):
                        last = nc.tensor.transpose(ps[:, c * P:(c + 1) * P], (x_in, x_res)[n][:, idx, c * P:(c + 1) * P],
                                                   ident)
                elif kind == "down":
                    te.wait_ge(h_lo, (i - 1) * FC + FC - 1)
                    head = SCORES_AT if idx == 0 else MS_AT if is_body(i, NG - 1) else 0
                    if head:
                        token_major(ps[:], h_t, idx, wd_t, 0, FC, range(head))
                    if idx == 0:
                        scores(0, i, range(HG // 2, HG))
                    elif head:
                        use(k + 1, i)
                    token_major(ps[:], h_t, idx, wd_t, 0, FC, range(head, FC - 1))
                    te.wait_ge(h_lo, (i - 1) * FC + FC)
                    last = token_major(ps[:], h_t, idx, wd_t, 0, FC, range(FC - 1, FC))
                elif kind == "st":
                    te.wait_ge(freed["kt"], val("kt", i, 0, idx))
                    for g in range(HG):
                        last = nc.tensor.matmul(ps[:, g * P:(g + 1) * P], k_dec[:, g * P:(g + 1) * P],
                                                v[:, idx, g * P:(g + 1) * P], start=True, stop=True,
                                                skip_group_check=True)
                elif kind in ("q", "k", "u"):
                    te.wait_ge(freed["ln1"], val("ln1", i, 1, 1))
                    base = {"q": 0, "k": D, "u": 3 * D}[kind] + idx * 2 * P
                    for half in range(2):
                        last = feature_major(ps[:, half * GT:(half + 1) * GT], wq_t, xn_t, base + half * P)
                elif kind == "v":
                    te.wait_ge(freed["ln1"], val("ln1", i, 1, 1))
                    last = token_major(ps[:], xn_t, idx, wq_t, 2 * D, DC)
                elif kind == "ms":
                    te.wait_ge(o_sq_sum, i + 1)
                    nc.tensor.matmul(ps[:, 0:GT], ones[:], rms[:, 0, :], start=True, stop=True)
                    for b in range(TB):
                        last = nc.tensor.matmul(ps[:, GT + b:GT + b + 1], rms[:, 0, b * C:(b + 1) * C], ones[:, 0:1],
                                                start=True, stop=True, skip_group_check=True)
                elif kind == "wo":
                    te.wait_ge(g_lo, TB * i + idx + 1)
                    last = token_major(ps[:], g_t, idx, wo_t, 0, DC)
                elif kind == "gu":
                    te.wait_ge(freed["ln2"], val("ln2", i, 0, 1))
                    feature_major(ps[:, 0:GT], wg_t, g_t, idx * P)
                    last = feature_major(ps[:, GT:2 * GT], wu_t, g_t, idx * P)
                last.then_inc(pe[kind], 1)

            def scores(b, i, groups):
                if not present(i, 0):
                    return
                te.wait_ge(freed["q"], val("q", i, 0, 1))
                if b > 0 or not is_body(i, 0):
                    te.wait_ge(probs_done, TB * i + b)
                tok = slice(b * C, (b + 1) * C)
                for g in groups:
                    for j in range(HPG):
                        rows = slice(j * DH, (j + 1) * DH)
                        last = nc.tensor.matmul(sc_ps[j][:, g * C:(g + 1) * C], k_t[rows, g, tok], q_t[rows, g, tok],
                                                start=True, stop=True, skip_group_check=True)
                if g == HG - 1:
                    last.then_inc(pe_scores, 1)

            def outputs(b, i):
                if not present(i, 0):
                    return
                te.wait_ge(q_dec_done, TB * i + b + 1)
                if not (isinstance(i, int) and i == 0):
                    te.wait_ge(st_done, TB * (i - 1) + b + 1)
                if b > 0 or not (isinstance(i, int) and i == 0):
                    te.wait_ge(o_read, TB * i + b)
                for g in range(HG):
                    nc.tensor.matmul(o_ps[:, g * C:(g + 1) * C], state[:, b, g, :], q_dec[:, g, :],
                                     start=(g == 0), stop=False, skip_group_check=True)
                te.wait_ge(probs_done, TB * i + b + 1)
                te.wait_ge(freed["v"], val("v", i, 0, 1))
                for g in range(HG):
                    for j in range(HPG):
                        last = nc.tensor.matmul(o_ps[j * DH:(j + 1) * DH, g * C:(g + 1) * C],
                                                v[:, b, g * P + j * DH:g * P + (j + 1) * DH],
                                                probs[:, j, g * C:(g + 1) * C], start=False, stop=True,
                                                skip_group_check=True)
                last.then_inc(pe_o, 1)

            def body(i):
                for k, (kind, idx, off) in enumerate(RING):
                    if kind == "ms" and is_body(i, NG - 1):
                        continue
                    if kind == "st":
                        outputs(idx, i)
                    use(k, i)
                    if (kind, idx) == ("kt", 0):
                        scores(0, i, range(HG // 2 if present(i, -1) else HG))
                    if (kind, idx) == ("kt", 1):
                        scores(1, i, range(HG // 2))
                    if (kind, idx) == ("q", 0):
                        scores(1, i, range(HG // 2, HG))
                    if k == 0 and is_body(i, 0):
                        te.wait_ge(sc_ready, 4)
                        te.wait_ge(row_copied, ROUNDS["o"])
                        te.wait_ge(freed["v"], TB)
                        te.wait_ge(freed["u"], 2)
                        row_table(h_unit, FC, (o_ps, main[1], main[2]))
                        te.wait_ge(row_copied, ROUNDS["h"])
                if is_body(i, -1):
                    for g in range(FIRST["g"] + 1, FIRST["d"]):
                        transpose_rows(g)
                        if g == FIRST["o"]:
                            te.wait_ge(scales_ready, g + 1)
                            row_table(pw_o, DC)
                    te.wait_ge(weights_lo, SETS_BEFORE[FIRST["d"]])
                if is_body(i, 0):
                    te.wait_ge(sc_ready, 5)
                    te.wait_ge(o_read, TB)
                    row_table(pw_d, DC)
                    te.wait_ge(row_copied, ROUNDS["d"])
                    te.wait_ge(weights_lo, len(SETS))

            over(te, body)

        @block.scalar
        def _(act):
            def decay_tables(part):
                if part == 0:
                    act.wait_ge(slopes_ready, 1)
                for j in ((0, 1), (2, 3), ())[part]:
                    for g in range(HG):
                        h = g * HPG + j
                        nc.scalar.activation(decay[:, j, g, :], rel, ACT.Exp, scale=nslope[:, h:h + 1])
                if part == 2:
                    for g in range(HG):
                        nc.scalar.activation(q_decay[:, g, :], scst[:, S_POS:S_POS + P], ACT.Exp,
                                             scale=nslope[:, H + g:H + g + 1])
                    nc.scalar.activation(chunk_decay[:], nslope[:, H:H + HG], ACT.Exp, scale=float(C))
                    nc.scalar.activation(k_decay[:], nslope[:, 0:H], ACT.Exp,
                                         scale=cst[:, C_REV:C_REV + 1]).then_inc(act_tables, 1)

            rounds = [0]

            def copy_table(dst, cols, banks=(o_ps,), scale=1.0):
                for n, c0 in enumerate(range(0, cols, 4)):
                    m = min(4, cols - c0)
                    rounds[0] += 1
                    act.wait_ge(row_made, rounds[0])
                    nc.scalar.activation(dst[:, c0 * P:(c0 + m) * P], banks[n % len(banks)][:, 0:m * P], ACT.Copy,
                                         scale=scale).then_inc(row_copied, 1)

            def hi_parts(gi):
                _, _, dst, _, t0, _ = GROUPS[gi]
                for n in sets_of(gi):
                    _, t, b0, nb = SETS[n]
                    act.wait_ge(rows_transposed, n + 1)
                    o0 = (t0 + t) * P
                    nc.scalar.activation(dst[0][:, b0:b0 + nb, o0:o0 + P],
                                         sc_ps[n % HPG][:, 0:nb * P].rearrange("p (b o) -> p b o", b=nb),
                                         ACT.Copy, scale=W_UP).then_inc(weights_hi, 1)

            def body(i):
                def product_silus(kind):
                    if not present(i, 1):
                        return
                    dst, base = (q_t, 0) if kind == "q" else (k_t, 4)
                    if is_body(i, -1):
                        if kind == "q":
                            hi_parts(0)
                        hi_parts(1 if kind == "q" else 2)
                        act.wait_ge(sc_ready, 1 if kind == "q" else 2)
                    for idx in range(2):
                        k = RING.index((kind, idx, 1))
                        act.wait_ge(pe[kind], val(kind, i, 1, idx))
                        if idx == 0 and not (isinstance(i, int) and i < 0):
                            act.wait_ge(pe_scores, TB * i + TB)
                            act.wait_ge(q_dec_done, TB * i + TB)
                        for half in range(2):
                            c = 2 * idx + half
                            last = nc.scalar.activation(dst[:, c, :], main[k % NBANK][:, half * GT:(half + 1) * GT],
                                                        ACT.Silu, scale=sc_qk[:, base + c:base + c + 1])
                        last.then_inc(freed[kind], 1)

                def output_out(b):
                    act.wait_ge(pe_o, TB * i + b + 1)
                    ops = o_ps[:].rearrange("p (g t) -> p g t", g=HG)
                    if b == 0 and not (isinstance(i, int) and i == 0):
                        act.wait_ge(g_lo, TB * i)
                    nc.scalar.activation(o_t[:, :, b * C:(b + 1) * C], ops, ACT.Copy).then_inc(o_read, 1)

                if present(i, 1):
                    for t in range(TB):
                        act.wait_ge(pe["ln1"], val("ln1", i, 1, t))
                        if t == 0 and not (isinstance(i, int) and i < 0):
                            act.wait_ge(pe["u"], val("u", i, 0, 1))
                        k = RING.index(("ln1", t, 1))
                        nc.scalar.activation(xn_t[0][:, :, t * C:(t + 1) * C],
                                             main[k % NBANK][:].rearrange("p (c t) -> p c t", c=DC),
                                             ACT.Copy, scale=X_UP).then_inc(ln1_hi, 1)
                if present(i, 0):
                    output_out(0)
                product_silus("q")
                if present(i, 0):
                    output_out(1)
                    act.wait_ge(pe_o, TB * i + TB)
                    act.wait_ge(o_read, TB * i + TB)
                    nc.scalar.activation(o_sq, o_t, ACT.Square).then_inc(o_sq_done, 1)
                if is_body(i, 0):
                    hi_parts(FIRST["d"])
                if present(i, 0):
                    for b in range(TB):
                        tok = slice(b * C, (b + 1) * C)
                        act.wait_ge(g_done, TB * i + b + 1)
                        if b == 0 and not (isinstance(i, int) and i == 0):
                            act.wait_ge(pe["gu"], val("gu", i, -1, FC - 1))
                        nc.scalar.activation(g_t[0][:, :, tok], o_t[:, :, tok], ACT.Copy).then_inc(g_hi, 1)
                product_silus("k")
                if is_body(i, -1):
                    copy_table(v_row, DC)
                    hi_parts(3)
                    copy_table(u_row, DC)
                    decay_tables(0)
                    hi_parts(4)
                    decay_tables(1)
                def u_out(idx):
                    if not present(i, 1):
                        return
                    k = RING.index(("u", idx, 1))
                    act.wait_ge(pe["u"], val("u", i, 1, idx))
                    if idx == 0 and not (isinstance(i, int) and i < 0):
                        act.wait_ge(ou_done, i + 1)
                    nc.scalar.activation(u_t[:, 2 * idx:2 * idx + 2, :],
                                         main[k % NBANK][:].rearrange("p (h t) -> p h t", h=2),
                                         ACT.Copy, scale=XW_DOWN).then_inc(freed["u"], 1)

                u_out(0)
                if is_body(i, -1):
                    u_out(1)
                    decay_tables(2)
                if is_body(i, -1):
                    for g in range(FIRST["g"] + 1, FIRST["d"]):
                        hi_parts(g)
                        if g == FIRST["o"]:
                            copy_table(o_row, DC, scale=1.0 / W_UP)
                    copy_table(h_row, FC, (o_ps, main[1], main[2]))
                if is_body(i, 0):
                    hi_parts(FIRST["d"] + 1)
                if present(i, 0):
                    for t in range(TB):
                        k = RING.index(("ln2", t, 0))
                        act.wait_ge(pe["ln2"], val("ln2", i, 0, t))
                        if t == 0:
                            act.wait_ge(pe["wo"], val("wo", i, 0, 1))
                        nc.scalar.activation(g_t[0][:, :, t * C:(t + 1) * C],
                                             main[k % NBANK][:].rearrange("p (c t) -> p c t", c=DC),
                                             ACT.Copy, scale=X_UP).then_inc(ln2_hi, 1)
                if not is_body(i, -1):
                    u_out(1)
                if present(i, 0):
                    if is_body(i, 0):
                        act.wait_ge(sc_ready, 4)

                    def hidden_hi(c):
                        act.wait_ge(h32_done, i * FC + c + 1)
                        if c == 0 and not (isinstance(i, int) and i == 0):
                            act.wait_ge(pe["down"], val("down", i, -1, 1))
                        nc.scalar.activation(h_t[0][:, c, :], h32[:, c % 2, :], ACT.Copy).then_inc(h_hi, 1)

                    for c in range(FC):
                        k = RING.index(("gu", c, 0))
                        act.wait_ge(pe["gu"], val("gu", i, 0, c))
                        nc.scalar.activation(silu_g[:, c % 2, :], main[k % NBANK][:, 0:GT], ACT.Silu,
                                             scale=sc_gate[:, c:c + 1]).then_inc(silu_done, 1)
                        if c >= 1:
                            hidden_hi(c - 1)
                        if is_body(i, 0) and c in (3, 7):
                            hi_parts(FIRST["d"] + 2 + c // 7)
                    hidden_hi(FC - 1)
                if is_body(i, 0):
                    copy_table(d_row, DC)

            over(act, body)

        @block.vector
        def _(dve):
            ts, tt, stt = nc.vector.tensor_scalar, nc.vector.tensor_tensor, nc.vector.scalar_tensor_tensor
            count = [0]

            def link(ins):
                count[0] += 1
                ins.then_inc(setup_chain, 1)
                dve.wait_ge(setup_chain, count[0])

            nc.vector.memset(state[:], 0.0)
            link(nc.vector.memset(ones[:], 1.0))

            def lo_parts(gi):
                _, _, dst, _, t0, _ = GROUPS[gi]
                for n in sets_of(gi):
                    _, t, b0, nb = SETS[n]
                    o0 = (t0 + t) * P
                    dve.wait_ge(weights_hi, n + 1)
                    stt(dst[1][:, b0:b0 + nb, o0:o0 + P],
                        sc_ps[n % HPG][:, 0:nb * P].rearrange("p (b o) -> p b o", b=nb), W_UP,
                        dst[0][:, b0:b0 + nb, o0:o0 + P], ALU.mult, ALU.subtract).then_inc(weights_lo, 1)

            def power_of_two(dst, src, inv):
                link(ts(dst, src, TINY, None, ALU.max))
                link(ts(dst.bitcast(I32), dst.bitcast(I32), EXPONENT, None, ALU.bitwise_and))
                return nc.vector.reciprocal(inv, dst)

            def row_scales(gi):
                name, _, _, pw, t0, tiles = GROUPS[gi]
                for t in range(tiles):
                    if name in "od":
                        dve.wait_ge(columns_scaled, t0 + t + 1 + (DC if name == "d" else 0))
                    else:
                        raw_loaded(dve, gi, t)
                    last = nc.vector.tensor_reduce(small[:, 3, t:t + 1], raw_tile(gi, t), axis=AX_X, op=ALU.max,
                                                   apply_absolute_value=True)
                link(last)
                if gi >= 2:
                    dve.wait_ge(rows_scaled, TILES_BEFORE[gi - 1])
                power_of_two(pw[:, t0:t0 + tiles], small[:, 3, 0:tiles], small[:, 4 + gi % 2, 0:tiles]).then_inc(scales_ready, 1)

            def decay_tables():
                dve.wait_ge(slopes_spread, 1)
                ts(nslope[:], o_ps[:, 0:H + HG], -1.0, None, ALU.mult).then_inc(slopes_ready, 1)

            def decay_mask():
                dve.wait_ge(act_tables, 1)
                tt(decay[:].rearrange("p j g m -> p (j g) m"), decay[:].rearrange("p j g m -> p (j g) m"),
                   mask.unsqueeze(1).to_broadcast([P, H, C]), ALU.mult).then_inc(tables_done, 1)

            def qkv_scales(g):
                ts(sc_qk[:, 4 * g:4 * g + 4], pw_q[:, 4 * g:4 * g + 4], XW_DOWN, None, ALU.mult).then_inc(sc_ready, 1)

            def ffn_scale_powers():
                dve.wait_ge(small_loaded, 48)
                for s in range(2):
                    link(ts(small[:, s, :].bitcast(I32), ffn_s[:, s, :].bitcast(I32), MAGNITUDE, None, ALU.bitwise_and))
                    link(power_of_two(small[:, s, :], small[:, s, :], small[:, 6 + s, :]))

            def ffn_scales():
                link(tt(small[:, 2, :], small[:, 0, :], small[:, 1, :], ALU.mult))
                link(tt(small[:, 2, :], small[:, 2, :], pw_g[:], ALU.mult))
                link(stt(h_unit[:], small[:, 2, :], 2.0 ** 7, pw_u[:], ALU.mult, ALU.mult))
                link(stt(sc_gate[:], pw_g[:], XW_DOWN, ffn_s[:, 0, :], ALU.mult, ALU.mult))
                link(nc.vector.reciprocal(small[:, 2, :], pw_g[:]))
                link(tt(small[:, 2, :], small[:, 2, :], small[:, 6, :], ALU.mult))
                link(tt(small[:, 2, :], small[:, 2, :], small[:, 7, :], ALU.mult))
                stt(sc_up[:], small[:, 2, :], XW_DOWN * 2.0 ** -7, ffn_s[:, 1, :], ALU.mult, ALU.mult).then_inc(sc_ready, 1)

            class Chain:

                def __init__(self, s, n, per):
                    self.s, self.n, self.per, self.k = s, n, per, 0

                def __call__(self, ins):
                    self.k += 1
                    ins.then_inc(self.s, 1)
                    dve.wait_ge(self.s, self.n * self.per + self.k)

                def end(self):
                    assert self.k == self.per

            def rsqrt_guess(link, y, t, vv):
                link(ts(t.bitcast(I32), vv.bitcast(I32), 1, None, ALU.logical_shift_right))
                link(ts(y.bitcast(I32), t.bitcast(I32), -1.0, RSQRT_SEED, ALU.mult, ALU.add))

            def rsqrt_steps(link, y, y0, t, vv):
                for n in range(3):
                    before = y0 if n == 0 else y
                    link(tt(t, before, before, ALU.mult))
                    link(stt(t, t, -0.5, vv, ALU.mult, ALU.mult))
                    link(stt(y, t, 1.5, before, ALU.add, ALU.mult))

            def layer_norm(which, src, dst, n, last):
                link = Chain(ln_chain[which], n, 14)
                st, m = stats[:, which], mv[:, which]
                link(last)
                nc.vector.memset(wait_slot[:], 0.0)
                for b in range(TB):
                    last = nc.vector.bn_aggr(m[:, b, :], st[:, b, :])
                link(last)
                vv, t, y = (ln_y[:, which, r, :] for r in range(3))
                link(ts(vv, m[:, :, 1], LN_EPS, None, ALU.add))
                rsqrt_guess(link, y, t, vv)
                rsqrt_steps(link, y, y, t, vv)
                link.end()
                for b in range(TB):
                    ts(dst[:, b, :], src[:, b, :], m[:, b, 0:1], y[:, b:b + 1],
                       ALU.subtract, ALU.mult).then_inc(ln_done[which], 1)

            def k_decayed(b, i):
                k = RING.index(("kt", b, 0))
                dve.wait_ge(pe["kt"], val("kt", i, 0, b))
                if b > 0 or not (isinstance(i, int) and i == 0):
                    dve.wait_ge(pe["st"], TB * i + b)
                tt(k_dec.rearrange("p (h d) -> p h d", h=H), main[k % NBANK][:].rearrange("p (h d) -> p h d", h=H),
                   k_decay[:].unsqueeze(2).to_broadcast([P, H, DH]), ALU.mult).then_inc(freed["kt"], 1)

            def q_decayed(b, i):
                dve.wait_ge(freed["q"], val("q", i, 0, 1))
                if b > 0 or not (isinstance(i, int) and i == 0):
                    dve.wait_ge(pe_o, TB * i + b)
                tt(q_dec, q_t[:, :, b * C:(b + 1) * C], q_decay[:], ALU.mult).then_inc(q_dec_done, 1)

            def weigh(b, i):
                dve.wait_ge(pe_scores, TB * i + b + 1)
                if b == 0 and is_body(i, 0):
                    dve.wait_ge(tables_done, 1)
                if not (isinstance(i, int) and i == 0) or b > 0:
                    dve.wait_ge(pe_o, TB * i + b)
                for j in range(HPG):
                    last = tt(probs[:, j, :], sc_ps[j][:], decay[:, j].rearrange("p g m -> p (g m)"), ALU.mult)
                last.then_inc(probs_done, 1)

            def new_state(b, i):
                k = RING.index(("st", b, 0))
                n = TB * i + b
                dve.wait_ge(pe["st"], n + 1)
                if b > 0:
                    dve.wait_ge(st_done, n)
                elif present(i, -1):
                    dve.wait_ge(final, TB * (i - 1) + 1)
                keep = cst[:, bass.ds(C_KEEP + i, 1)]
                stt(kv_new[:].rearrange("p (g e) -> p g e", g=HG), main[k % NBANK][:].rearrange("p (g e) -> p g e", g=HG),
                    keep, block_mask.unsqueeze(1).to_broadcast([P, HG, P]), ALU.mult, ALU.mult).then_inc(freed["st"], 1)
                stt(kv_old[:].rearrange("p (g e) -> p g e", g=HG), state[:, b], keep,
                    chunk_decay[:].unsqueeze(2).to_broadcast([P, HG, P]), ALU.mult, ALU.mult).then_inc(st_chain, 1)
                dve.wait_ge(st_chain, n + 1)
                tt(state[:, b].rearrange("p g e -> p (g e)"), kv_new[:], kv_old[:], ALU.add).then_inc(st_done, 1)

            def down_out(b, i):
                if not present(i, -1):
                    return
                k = RING.index(("down", b, -1))
                n = TB * (i - 1) + b
                dve.wait_ge(pe["down"], n + 1)
                if b == 0:
                    dve.wait_ge(res_added, TB * i)
                elif present(i, 0):
                    dve.wait_ge(st_done, TB * i + TB)
                else:
                    dve.wait_ge(final, n)
                tt(y_tmp[:], main[k % NBANK][:], d_row[:], ALU.mult).then_inc(freed["down"], 1)

            def down_added(b, i):
                if not present(i, -1):
                    return
                n = TB * (i - 1) + b
                dve.wait_ge(freed["down"], n + 1)
                tt(x2[:, b, :], x2[:, b, :], y_tmp[:], ALU.add).then_inc(final, 1)

            def token_parts(kind, dst, hi, i, off, t):
                k = RING.index((kind, t, off))
                dve.wait_ge(hi, val(kind, i, off, t))
                stt(dst[1][:, :, t * C:(t + 1) * C], main[k % NBANK][:].rearrange("p (c t) -> p c t", c=DC), X_UP,
                    dst[0][:, :, t * C:(t + 1) * C], ALU.mult, ALU.subtract).then_inc(freed[kind], 1)

            def v_out(idx, i):
                if not present(i, 1):
                    return
                k = RING.index(("v", idx, 1))
                dve.wait_ge(pe["v"], val("v", i, 1, idx))
                if idx == 0 and not (isinstance(i, int) and i < 0):
                    dve.wait_ge(pe["st"], TB * i + TB)
                if is_body(i, -1):
                    dve.wait_ge(row_copied, ROUNDS["v"])
                tt(v[:, idx, :], main[k % NBANK][:], v_row[:], ALU.mult).then_inc(freed["v"], 1)

            def body(i):
                if present(i, 0):
                    k_decayed(0, i)
                    q_decayed(0, i)
                if present(i, 1) and not is_body(i, 0):
                    dve.wait_ge(x_loaded, 16 * (i + 1) + 16)
                    for b in range(TB):
                        last = nc.vector.bn_stats(stats[:, 0, b, :], x_in[:, b, :])
                    layer_norm(0, x_in, x_in, i + 1, last)
                if present(i, 0):
                    weigh(0, i)
                down_out(0, i)
                down_added(0, i)
                if present(i, 1):
                    if is_body(i, -1):
                        row_scales(0)
                    for t in range(TB):
                        token_parts("ln1", xn_t, ln1_hi, i, 1, t)
                if present(i, 0):
                    new_state(0, i)
                    k_decayed(1, i)
                    q_decayed(1, i)
                    weigh(1, i)
                    if is_body(i, 0):
                        row_scales(FIRST["d"])
                if is_body(i, -1):
                    decay_tables()
                    row_scales(1)
                    qkv_scales(0)
                    lo_parts(0)
                    row_scales(2)
                    qkv_scales(1)
                    lo_parts(1)
                    row_scales(3)
                    qkv_scales(2)
                    lo_parts(2)
                    row_scales(4)
                    lo_parts(3)
                    ffn_scale_powers()
                    dve.wait_ge(x_loaded, 32)
                    dve.wait_ge(ln_done[0], TB)
                    for b in range(TB):
                        last = nc.vector.bn_stats(stats[:, 0, b, :], x_in[:, b, :])
                    layer_norm(0, x_in, x_in, 1, last)
                if present(i, 0):
                    new_state(1, i)
                    dve.wait_ge(o_sq_done, i + 1)
                    nc.vector.tensor_reduce(rms[:, 0, :], o_sq.rearrange("p h t -> p t h"), axis=AX_X,
                                            op=ALU.add).then_inc(o_sq_sum, 1)
                    dve.wait_ge(freed["u"], val("u", i, 0, 1))
                    dve.wait_ge(o_read, TB * i + TB)
                    tt(o_t, o_t, u_t, ALU.mult).then_inc(ou_done, 1)
                    step = Chain(g_chain, i, 2)
                    dve.wait_ge(pe["ms"], i + 1)
                    k = RING.index(("ms", 0, 0))
                    ts(rms[:, 1, :], main[k % NBANK][:, 0:GT], 1.0 / D, RMS_EPS, ALU.mult, ALU.add)
                    ts(rms_tok[:, 0, :], main[k % NBANK][:, GT:GT + TB], 1.0 / D, RMS_EPS,
                       ALU.mult, ALU.add).then_inc(freed["ms"], 1)
                    dve.wait_ge(freed["ms"], i + 1)
                    rsqrt_guess(step, rms[:, 3, :], rms[:, 2, :], rms[:, 1, :])
                    step.end()
                if not is_body(i, NG - 1):
                    down_out(1, i)
                if present(i, 0):
                    dve.wait_ge(ou_done, i + 1)
                    for b in range(TB):
                        tok = slice(b * C, (b + 1) * C)
                        tt(o_t[:, :, tok], o_t[:, :, tok], rms[:, 3, tok].unsqueeze(1).to_broadcast([P, HG, C]),
                           ALU.mult).then_inc(g_done, 1)
                if not is_body(i, NG - 1):
                    down_added(1, i)
                if present(i, 0):
                    for b in range(TB):
                        tok = slice(b * C, (b + 1) * C)
                        dve.wait_ge(g_hi, TB * i + b + 1)
                        tt(g_t[1][:, :, tok], o_t[:, :, tok], g_t[0][:, :, tok], ALU.subtract).then_inc(g_lo, 1)
                    if is_body(i, NG - 1):
                        down_out(1, i)
                        down_added(1, i)
                    step = Chain(rms_chain, i, 13)
                    vv, t, y, y0, f = (rms_tok[:, r, :] for r in range(5))
                    rsqrt_guess(step, y0, t, vv)
                    rsqrt_steps(step, y, y0, t, vv)
                    step(nc.vector.reciprocal(y0, y0))
                    step(tt(f, y, y0, ALU.mult))
                    step.end()
                    if is_body(i, 0):
                        row_scales(FIRST["d"] + 1)
                        lo_parts(FIRST["d"])
                    dve.wait_ge(res_loaded, 16 * i + 16)
                    for b in range(TB):
                        k = RING.index(("wo", b, 0))
                        dve.wait_ge(pe["wo"], val("wo", i, 0, b))
                        if b == 0 and present(i, -1):
                            dve.wait_ge(final, TB * (i - 1) + TB)
                        elif b == 0:
                            dve.wait_ge(st_done, TB * i + TB)
                        else:
                            dve.wait_ge(res_added, TB * i + b)
                        tt(y_tmp[:], main[k % NBANK][:], o_row[:], ALU.mult).then_inc(freed["wo"], 1)
                        dve.wait_ge(freed["wo"], val("wo", i, 0, b))
                        if b == 0 and not is_body(i, 0):
                            dve.wait_ge(stored, 16 * i)
                        stt(x2[:, b, :], y_tmp[:], f[:, b:b + 1], x_res[:, b, :], ALU.mult, ALU.add).then_inc(res_added, 1)
                        dve.wait_ge(res_added, TB * i + b + 1)
                        last = nc.vector.bn_stats(stats[:, 1, b, :], x2[:, b, :])
                    layer_norm(1, x2, x_res, i, last)
                for idx in range(TB):
                    v_out(idx, i)
                if is_body(i, -1):
                    for g in range(FIRST["g"] + 1, FIRST["d"]):
                        row_scales(g)
                        lo_parts(g - 1)
                    lo_parts(FIRST["d"] - 1)
                    ffn_scales()
                    decay_mask()
                    dve.wait_ge(row_copied, ROUNDS["o"])
                if is_body(i, 0):
                    lo_parts(FIRST["d"] + 1)
                if present(i, 0):
                    for t in range(TB):
                        token_parts("ln2", g_t, ln2_hi, i, 0, t)

                    def hidden_lo(c):
                        dve.wait_ge(h_hi, i * FC + c + 1)
                        tt(h_t[1][:, c, :], h32[:, c % 2, :], h_t[0][:, c, :], ALU.subtract).then_inc(h_lo, 1)

                    for c in range(FC):
                        k = RING.index(("gu", c, 0))
                        dve.wait_ge(silu_done, i * FC + c + 1)
                        if c >= 2 or not is_body(i, 0):
                            dve.wait_ge(h_lo, i * FC + max(c - 1, 0))
                        stt(h32[:, c % 2, :], main[k % NBANK][:, GT:2 * GT], sc_up[:, c:c + 1],
                            silu_g[:, c % 2, :], ALU.mult, ALU.mult).then_inc(h32_done, 1)
                        if c >= 1:
                            hidden_lo(c - 1)
                        if is_body(i, 0):
                            if c == 1:
                                row_scales(FIRST["d"] + 2)
                            if c == 4:
                                row_scales(FIRST["d"] + 3)
                                lo_parts(FIRST["d"] + 2)
                            if c == 8:
                                lo_parts(FIRST["d"] + 3)
                    hidden_lo(FC - 1)
                if is_body(i, 0):
                    stt(pw_d[:], pw_d[:], 1.0 / W_UP, down_sc[:], ALU.mult, ALU.mult).then_inc(sc_ready, 1)
                    dve.wait_ge(row_copied, ROUNDS["d"])

            over(dve, body)

        @block.gpsimd
        def _(pool):
            def column_scales(gi):
                name, tiles = GROUPS[gi][0], GROUPS[gi][5]
                pool.wait_ge(row_copied, ROUNDS["u" if name == "o" else "h"])
                for t in range(tiles):
                    raw_loaded(pool, gi, t)
                    nc.gpsimd.tensor_tensor(raw_tile(gi, t), raw_tile(gi, t), u_row if name == "o" else h_row[:],
                                            ALU.mult).then_inc(columns_scaled, 1)

            for gi, (name, _, _, _, t0, tiles) in enumerate(GROUPS):
                if gi + 1 == FIRST["o"]:
                    column_scales(FIRST["o"])
                if name == "d":
                    column_scales(gi)
                pool.wait_ge(scales_ready, gi + 1)
                for t in range(tiles):
                    nc.gpsimd.tensor_scalar(raw_tile(gi, t), raw_tile(gi, t), small[:, 4 + gi % 2, t:t + 1], 1.0,
                                            ALU.mult, ALU.mult).then_inc(rows_scaled, 1)


NAMES = {"L0_attn_x": "x", "L0_attn_slope_rate": "slope", "L0_attn_W_qkvu": "w_qkvu", "L0_attn_W_out": "w_out",
         "L0_ffn_gate_w": "gate_w", "L0_ffn_up_w": "up_w", "L0_ffn_down_w": "down_w",
         "L0_ffn_gate_s": "gate_s", "L0_ffn_up_s": "up_s", "L0_ffn_down_s": "down_s"}


def kernel(**inputs):
    import numpy as np
    import concourse.bacc as bacc
    from concourse.bass_utils import run_bass_kernel_spmd

    nc = bacc.Bacc("TRN2", target_bir_lowering=False, num_devices=1)
    arrays = {}
    for name, short in NAMES.items():
        arrays[f"in_{short}"] = np.ascontiguousarray(inputs[name])
    pos = np.arange(P)
    consts = np.zeros((P, N_CONST), np.float32)
    consts[:, C_IDENT:C_IDENT + P] = np.eye(P)
    consts[:, C_BLOCK:C_BLOCK + P] = pos[None, :] // DH == pos[:, None] // DH
    consts[:, C_REV] = C - 1 - pos
    consts[:, C_KEEP:C_KEEP + NG] = np.arange(NG)[None, :] % NC != NC - 1
    setup_consts = np.zeros((P, N_SETUP), np.float32)
    setup_consts[:, S_REL:S_REL + P] = np.maximum(pos[None, :] - pos[:, None], 0)
    setup_consts[:, S_MASK:S_MASK + P] = pos[None, :] >= pos[:, None]
    setup_consts[:, S_POS:S_POS + P] = pos[None, :] + 1
    setup_consts[0:HPG, S_HEAD:S_HEAD + P] = pos[None, :] // DH == np.arange(HPG)[:, None]
    arrays["in_consts"] = consts
    arrays["in_setup_consts"] = setup_consts
    aps = {n: nc.dram_tensor(n, a.shape, mybir.dt.from_np(a.dtype), kind="ExternalInput").ap()
           for n, a in arrays.items()}
    out = nc.dram_tensor("out", (B, T, D), F32, kind="ExternalOutput").ap()
    build_program(nc, *(aps[f"in_{s}"] for s in NAMES.values()), aps["in_consts"],
                  aps["in_setup_consts"], out)
    r = run_bass_kernel_spmd(nc, [arrays], core_ids=[0])
    return r.results[0]["out"]
```
